# Optimizing a Trainium2 kernel written in Bass

```python
import numpy as np
import jax
import jax.numpy as jnp

def _softmax(x, axis=-1):
    return jax.nn.softmax(x, axis=axis)

def _gelu(x):
    return jax.nn.gelu(x, approximate=True)

def _silu(x):
    return jax.nn.silu(x)

def _sigmoid(x):
    return jax.nn.sigmoid(x)

def _layernorm(x, axis=-1, eps=1e-05):
    m = jnp.mean(x, axis=axis, keepdims=True)
    v = jnp.var(x, axis=axis, keepdims=True)
    return (x - m) / jnp.sqrt(v + eps)

def _scatter_add(tgt, idx, src, axis=0):
    return tgt.at[idx].add(src)

def _segment_sum(src, seg, n):
    return jax.ops.segment_sum(src, seg, n)
kernel_name = 'mk_dlrm_tower_d1_rec_r8_b2b877'

def setup_inputs(seed: int=0):
    np.random.seed(seed)
    _w = jnp.asarray

    def _rec_inputs():
        import jax
        import jax.numpy as jnp
        _tk = jax.random.key(seed)
        dense_ctx = jax.random.normal(jax.random.fold_in(_tk, 190), (512, 16), jnp.float32)
        ids = jnp.stack([jax.random.randint(jax.random.fold_in(_tk, 200 + f), (512,), 0, v, jnp.int32) for f, v in enumerate([125000, 1250, 125000, 125000, 1250, 12500, 1250, 1000, 12500, 125000, 1000, 125000, 12500, 1000, 1000, 1000, 1250, 12500, 125000, 1250, 125000, 1000, 1250, 1000, 1250, 1250, 1250, 1250, 12500, 1000, 1250, 1000])], axis=1)
        tbl_0 = 0.05 * jax.random.normal(jax.random.fold_in(_tk, 500 + 0), (125000, 16), jnp.float32)
        tbl_1 = 0.05 * jax.random.normal(jax.random.fold_in(_tk, 500 + 1), (1250, 16), jnp.float32)
        tbl_2 = 0.05 * jax.random.normal(jax.random.fold_in(_tk, 500 + 2), (125000, 16), jnp.float32)
        tbl_3 = 0.05 * jax.random.normal(jax.random.fold_in(_tk, 500 + 3), (125000, 16), jnp.float32)
        tbl_4 = 0.05 * jax.random.normal(jax.random.fold_in(_tk, 500 + 4), (1250, 16), jnp.float32)
        tbl_5 = 0.05 * jax.random.normal(jax.random.fold_in(_tk, 500 + 5), (12500, 16), jnp.float32)
        tbl_6 = 0.05 * jax.random.normal(jax.random.fold_in(_tk, 500 + 6), (1250, 16), jnp.float32)
        tbl_7 = 0.05 * jax.random.normal(jax.random.fold_in(_tk, 500 + 7), (1000, 16), jnp.float32)
        tbl_8 = 0.05 * jax.random.normal(jax.random.fold_in(_tk, 500 + 8), (12500, 16), jnp.float32)
        tbl_9 = 0.05 * jax.random.normal(jax.random.fold_in(_tk, 500 + 9), (125000, 16), jnp.float32)
        tbl_10 = 0.05 * jax.random.normal(jax.random.fold_in(_tk, 500 + 10), (1000, 16), jnp.float32)
        tbl_11 = 0.05 * jax.random.normal(jax.random.fold_in(_tk, 500 + 11), (125000, 16), jnp.float32)
        tbl_12 = 0.05 * jax.random.normal(jax.random.fold_in(_tk, 500 + 12), (12500, 16), jnp.float32)
        tbl_13 = 0.05 * jax.random.normal(jax.random.fold_in(_tk, 500 + 13), (1000, 16), jnp.float32)
        tbl_14 = 0.05 * jax.random.normal(jax.random.fold_in(_tk, 500 + 14), (1000, 16), jnp.float32)
        tbl_15 = 0.05 * jax.random.normal(jax.random.fold_in(_tk, 500 + 15), (1000, 16), jnp.float32)
        tbl_16 = 0.05 * jax.random.normal(jax.random.fold_in(_tk, 500 + 16), (1250, 16), jnp.float32)
        tbl_17 = 0.05 * jax.random.normal(jax.random.fold_in(_tk, 500 + 17), (12500, 16), jnp.float32)
        tbl_18 = 0.05 * jax.random.normal(jax.random.fold_in(_tk, 500 + 18), (125000, 16), jnp.float32)
        tbl_19 = 0.05 * jax.random.normal(jax.random.fold_in(_tk, 500 + 19), (1250, 16), jnp.float32)
        tbl_20 = 0.05 * jax.random.normal(jax.random.fold_in(_tk, 500 + 20), (125000, 16), jnp.float32)
        tbl_21 = 0.05 * jax.random.normal(jax.random.fold_in(_tk, 500 + 21), (1000, 16), jnp.float32)
        tbl_22 = 0.05 * jax.random.normal(jax.random.fold_in(_tk, 500 + 22), (1250, 16), jnp.float32)
        tbl_23 = 0.05 * jax.random.normal(jax.random.fold_in(_tk, 500 + 23), (1000, 16), jnp.float32)
        tbl_24 = 0.05 * jax.random.normal(jax.random.fold_in(_tk, 500 + 24), (1250, 16), jnp.float32)
        tbl_25 = 0.05 * jax.random.normal(jax.random.fold_in(_tk, 500 + 25), (1250, 16), jnp.float32)
        tbl_26 = 0.05 * jax.random.normal(jax.random.fold_in(_tk, 500 + 26), (1250, 16), jnp.float32)
        tbl_27 = 0.05 * jax.random.normal(jax.random.fold_in(_tk, 500 + 27), (1250, 16), jnp.float32)
        tbl_28 = 0.05 * jax.random.normal(jax.random.fold_in(_tk, 500 + 28), (12500, 16), jnp.float32)
        tbl_29 = 0.05 * jax.random.normal(jax.random.fold_in(_tk, 500 + 29), (1000, 16), jnp.float32)
        tbl_30 = 0.05 * jax.random.normal(jax.random.fold_in(_tk, 500 + 30), (1250, 16), jnp.float32)
        tbl_31 = 0.05 * jax.random.normal(jax.random.fold_in(_tk, 500 + 31), (1000, 16), jnp.float32)
        _rk = jax.random.fold_in(_tk, 7)
        W_top1 = 0.0693375 * jax.random.normal(jax.random.fold_in(_tk, 801), (208, 512), jnp.float32)
        W_top2 = 0.0441942 * jax.random.normal(jax.random.fold_in(_tk, 802), (512, 256), jnp.float32)
        W_top3 = 0.0625 * jax.random.normal(jax.random.fold_in(_tk, 803), (256, 1), jnp.float32)
        b_top1 = jnp.zeros((512,), jnp.float32)
        b_top2 = jnp.zeros((256,), jnp.float32)
        return (dense_ctx, ids, tbl_0, tbl_1, tbl_2, tbl_3, tbl_4, tbl_5, tbl_6, tbl_7, tbl_8, tbl_9, tbl_10, tbl_11, tbl_12, tbl_13, tbl_14, tbl_15, tbl_16, tbl_17, tbl_18, tbl_19, tbl_20, tbl_21, tbl_22, tbl_23, tbl_24, tbl_25, tbl_26, tbl_27, tbl_28, tbl_29, tbl_30, tbl_31, W_top1, b_top1, W_top2, b_top2, W_top3)
    dense_ctx, ids, tbl_0, tbl_1, tbl_2, tbl_3, tbl_4, tbl_5, tbl_6, tbl_7, tbl_8, tbl_9, tbl_10, tbl_11, tbl_12, tbl_13, tbl_14, tbl_15, tbl_16, tbl_17, tbl_18, tbl_19, tbl_20, tbl_21, tbl_22, tbl_23, tbl_24, tbl_25, tbl_26, tbl_27, tbl_28, tbl_29, tbl_30, tbl_31, W_top1, b_top1, W_top2, b_top2, W_top3 = _rec_inputs()

    def _L0_rec_setup():
        import jax, jax.numpy as jnp
        import numpy as np
        B, M, D = (2048, 32, 16)
        LAYERS = [64, 64, 64]
        key = jax.random.key(seed)
        ks = jax.random.split(key, 4)
        inp = {'embeddings': jax.random.normal(ks[0], (B, M, D), dtype=jnp.float32)}
        hk_1 = M
        for i, hk in enumerate(LAYERS):
            scale = (2.0 / (M * hk_1 + hk)) ** 0.5
            inp[f'W{i}'] = jax.random.normal(ks[i + 1], (M, hk_1, hk), dtype=jnp.float32) * scale
            hk_1 = hk
        return inp
    _L0_rec_all = _L0_rec_setup()
    _L0_rec_in = {k: v for k, v in _L0_rec_all.items() if k in ('W0', 'W1', 'W2')}
    del _L0_rec_all
    return {'dense_ctx': dense_ctx, 'ids': ids, 'tbl_0': tbl_0, 'tbl_1': tbl_1, 'tbl_2': tbl_2, 'tbl_3': tbl_3, 'tbl_4': tbl_4, 'tbl_5': tbl_5, 'tbl_6': tbl_6, 'tbl_7': tbl_7, 'tbl_8': tbl_8, 'tbl_9': tbl_9, 'tbl_10': tbl_10, 'tbl_11': tbl_11, 'tbl_12': tbl_12, 'tbl_13': tbl_13, 'tbl_14': tbl_14, 'tbl_15': tbl_15, 'tbl_16': tbl_16, 'tbl_17': tbl_17, 'tbl_18': tbl_18, 'tbl_19': tbl_19, 'tbl_20': tbl_20, 'tbl_21': tbl_21, 'tbl_22': tbl_22, 'tbl_23': tbl_23, 'tbl_24': tbl_24, 'tbl_25': tbl_25, 'tbl_26': tbl_26, 'tbl_27': tbl_27, 'tbl_28': tbl_28, 'tbl_29': tbl_29, 'tbl_30': tbl_30, 'tbl_31': tbl_31, 'W_top1': W_top1, 'b_top1': b_top1, 'W_top2': W_top2, 'b_top2': b_top2, 'W_top3': W_top3, 'L0_rec_W0': _L0_rec_in['W0'], 'L0_rec_W1': _L0_rec_in['W1'], 'L0_rec_W2': _L0_rec_in['W2']}

def reference(dense_ctx, ids, tbl_0, tbl_1, tbl_2, tbl_3, tbl_4, tbl_5, tbl_6, tbl_7, tbl_8, tbl_9, tbl_10, tbl_11, tbl_12, tbl_13, tbl_14, tbl_15, tbl_16, tbl_17, tbl_18, tbl_19, tbl_20, tbl_21, tbl_22, tbl_23, tbl_24, tbl_25, tbl_26, tbl_27, tbl_28, tbl_29, tbl_30, tbl_31, W_top1, b_top1, W_top2, b_top2, W_top3, L0_rec_W0, L0_rec_W1, L0_rec_W2):
    import jax
    import jax.numpy as jnp

    def _L0_rec_ref(embeddings, W0, W1, W2):
        import jax, jax.numpy as jnp
        import numpy as np
        B, M, D = (2048, 32, 16)
        LAYERS = [64, 64, 64]
        x0 = embeddings
        xk = x0
        outs = []
        for W in (W0, W1, W2):
            xk = jax.nn.relu(jnp.einsum('bmd,bhd,mhk->bkd', x0, xk, W))
            outs.append(jnp.sum(xk, axis=2))
        return jnp.concatenate(outs, axis=1)
    e = jnp.stack([tbl_0[ids[:, 0]], tbl_1[ids[:, 1]], tbl_2[ids[:, 2]], tbl_3[ids[:, 3]], tbl_4[ids[:, 4]], tbl_5[ids[:, 5]], tbl_6[ids[:, 6]], tbl_7[ids[:, 7]], tbl_8[ids[:, 8]], tbl_9[ids[:, 9]], tbl_10[ids[:, 10]], tbl_11[ids[:, 11]], tbl_12[ids[:, 12]], tbl_13[ids[:, 13]], tbl_14[ids[:, 14]], tbl_15[ids[:, 15]], tbl_16[ids[:, 16]], tbl_17[ids[:, 17]], tbl_18[ids[:, 18]], tbl_19[ids[:, 19]], tbl_20[ids[:, 20]], tbl_21[ids[:, 21]], tbl_22[ids[:, 22]], tbl_23[ids[:, 23]], tbl_24[ids[:, 24]], tbl_25[ids[:, 25]], tbl_26[ids[:, 26]], tbl_27[ids[:, 27]], tbl_28[ids[:, 28]], tbl_29[ids[:, 29]], tbl_30[ids[:, 30]], tbl_31[ids[:, 31]]], axis=1)
    z = _L0_rec_ref(e, L0_rec_W0, L0_rec_W1, L0_rec_W2)
    z = z.reshape(z.shape[0], -1)
    h = jnp.concatenate([z, dense_ctx], axis=1)
    h = jnp.maximum(h @ W_top1 + b_top1, 0.0)
    h = jnp.maximum(h @ W_top2 + b_top2, 0.0)
    y = h @ W_top3
    return y

_drawn_inputs = setup_inputs


def setup_inputs(seed=0):
    import zlib

    import numpy as np

    out = dict(_drawn_inputs(seed))
    spreads = {'b_top1': (0.0, 2.0), 'b_top2': (0.0, 0.8)}
    factors = {'tbl_0': 8.0,
     'tbl_1': 8.0,
     'tbl_2': 8.0,
     'tbl_3': 8.0,
     'tbl_4': 8.0,
     'tbl_5': 8.0,
     'tbl_6': 8.0,
     'tbl_7': 8.0,
     'tbl_8': 8.0,
     'tbl_9': 8.0,
     'tbl_10': 8.0,
     'tbl_11': 8.0,
     'tbl_12': 8.0,
     'tbl_13': 8.0,
     'tbl_14': 8.0,
     'tbl_15': 8.0,
     'tbl_16': 8.0,
     'tbl_17': 8.0,
     'tbl_18': 8.0,
     'tbl_19': 8.0,
     'tbl_20': 8.0,
     'tbl_21': 8.0,
     'tbl_22': 8.0,
     'tbl_23': 8.0,
     'tbl_24': 8.0,
     'tbl_25': 8.0,
     'tbl_26': 8.0,
     'tbl_27': 8.0,
     'tbl_28': 8.0,
     'tbl_29': 8.0,
     'tbl_30': 8.0,
     'tbl_31': 8.0,
     'L0_rec_W0': 3.596,
     'L0_rec_W1': 8.0,
     'L0_rec_W2': 8.0,
     'dense_ctx': 7.472}
    for name, (base, spread) in spreads.items():
        noise = np.random.default_rng([zlib.crc32(name.encode()), seed]).standard_normal(out[name].shape)
        drawn = base * np.exp(spread * noise) if base else spread * noise
        out[name] = jnp.asarray(drawn.astype(out[name].dtype))
    for name, factor in factors.items():
        out[name] = (out[name] * factor).astype(out[name].dtype)
    return out
```

```python
from contextlib import ExitStack

import numpy as np

import concourse.bass as bass
from concourse import mybir

F32 = mybir.dt.float32
I32 = mybir.dt.int32
ALU = mybir.AluOpType
ACT = mybir.ActivationFunctionType
AXIS = mybir.AxisListType

B, M, D, K = 512, 32, 16, 64
TB = 32
C = TB * D
NP = B // (2 * TB)
NI, NJ = M // 8, K // 16
JV = NJ - 1
NH = M // 16
G = M // 4
UNITS = 4
SLOTS = 3
H1, H2 = 512, 256
N1, N2 = H1 // 128, H2 // 128


COUNT_0 = (0, 0, 1)


def vector_units_before(p):
    return 3 * UNITS * p - 2 * UNITS


def pool_units_before(p):
    return 2 * UNITS * p - 2 * UNITS


def build(nc, table, ids, base, w0, w0_mirror, w12, dense, w_top1, b_top1, w_top2, b_top2, w_top3, out):
    x0_dram = nc.dram_tensor("x0_rows", (2, M, C), F32).ap()
    x_dram = [nc.dram_tensor(f"x{n + 1}_rows", (2 * K, C), F32).ap() for n in range(2)]

    with ExitStack() as ctx:
        def sb(name, shape, dt=F32):
            return ctx.enter_context(nc.sbuf_tensor(name, shape, dt))

        def sem(name):
            return ctx.enter_context(nc.semaphore(name))

        ids_all = sb("ids_all", [128, NP, 2 * G], I32)
        table_base = sb("table_base", [128, 2 * G], I32)
        row_index = sb("row_index", [128, 2 * G], I32)
        gathered_rows = [sb(f"gathered_rows{n}", [128, 2, G, D]) for n in range(2)]
        x0_forms = sb("x0_forms", [128, SLOTS, 2, NI, C])
        h_forms = sb("h_forms", [128, 2, NH, C])
        x_forms = [sb(f"x{n + 1}_forms", [128, 2, NJ, C]) for n in range(2)]
        z_vector = sb("z_vector", [128, UNITS, JV * 2, C])
        z_pool = sb("z_pool", [128, UNITS, 2, C])
        w0_plain = sb("w0_plain", [128, 6, K])
        w0_extra = sb("w0_extra", [128, 2, K])
        w12_sb = sb("w12_sb", [128, 2, NJ, NI, K])
        x_sb = [sb(f"x{n + 1}_sb", [128, C]) for n in range(3)]
        d_sums = sb("d_sums", [128, 3, NP * TB])
        dense_sb = sb("dense_sb", [128, NP * TB])
        w_top1_sb = sb("w_top1_sb", [128, 3, H1])
        w_dense_sb = sb("w_dense_sb", [128, H1])
        w_top2_sb = sb("w_top2_sb", [128, N1, H2])
        w_top3_sb = sb("w_top3_sb", [128, N2])
        b_top1_sb = sb("b_top1_sb", [128, N1])
        b_top2_sb = sb("b_top2_sb", [128, N2])
        hidden1 = sb("hidden1", [128, N1, B])
        hidden2 = sb("hidden2", [128, N2, B])
        y_sb = sb("y_sb", [1, B])

        x0_psum = ctx.enter_context(nc.psum_tensor("x0_psum", [128, 2, 2, C], F32))
        result = [ctx.enter_context(nc.psum_tensor(f"result{n}", [128, C], F32)) for n in range(3)]
        y_psum = ctx.enter_context(nc.psum_tensor("y_psum", [128, B], F32))
        top1_psum = x0_psum[:].rearrange("p t i (n c) -> p t (i n) c", n=2)

        ids_loaded = sem("ids_loaded")
        w0_loaded = sem("w0_loaded")
        w12_loaded = sem("w12_loaded")
        top_loaded = sem("top_loaded")
        w0_folded = sem("w0_folded")
        index_ready = sem("index_ready")
        gathers_begun = sem("gathers_begun")
        rows_gathered = sem("rows_gathered")
        x0_stored = sem("x0_stored")
        x0_loaded = sem("x0_loaded")
        h_loaded = sem("h_loaded")
        x_stored = [sem(f"x{n + 1}_stored") for n in range(2)]
        x_loaded = [sem(f"x{n + 1}_loaded") for n in range(2)]
        x0_copied = sem("x0_copied")
        z_vector_ready = sem("z_vector_ready")
        z_vector_used = sem("z_vector_used")
        z_pool_ready = sem("z_pool_ready")
        z_pool_used = sem("z_pool_used")
        x_ready = [sem(f"x{n + 1}_ready") for n in range(3)]
        x_summed = [sem(f"x{n + 1}_summed") for n in range(3)]
        hidden1_summed = sem("hidden1_summed")
        hidden1_ready = sem("hidden1_ready")
        hidden2_summed = sem("hidden2_summed")
        hidden2_ready = sem("hidden2_ready")
        y_summed = sem("y_summed")
        y_ready = sem("y_ready")
        y_stored = sem("y_stored")

        block = ctx.enter_context(nc.Block())

        @block.sync
        def _(sp):
            def store_x0(there, rows):
                sp.wait_ge(rows_gathered, there)
                for t in range(2):
                    sp.dma_start(x0_dram[t].rearrange("(g m) (b d) -> (m b) g d", m=4, d=D),
                                 rows[:, t]).then_inc(x0_stored, 16)

            def load_x0(stored, slot):
                sp.wait_ge(x0_stored, stored)
                for t in range(2):
                    for j in range(NH):
                        sp.dma_start(h_forms[:, t, j],
                                     x0_dram[t, 16 * j:16 * j + 16].unsqueeze(0).broadcast_to([8, 16, C])
                                     ).then_inc(h_loaded, 16)
                for i in range(NI):
                    for t in range(2):
                        sp.dma_start(x0_forms[:, slot, t, i],
                                     x0_dram[t, 8 * i:8 * i + 8].unsqueeze(1).broadcast_to([8, 16, C])
                                     ).then_inc(x0_loaded, 16)

            def store_x(n, pairs):
                sp.wait_ge(x_ready[n], pairs)
                sp.dma_start(x_dram[n], x_sb[n][:]).then_inc(x_stored[n], 16)

            def load_x(n, stored):
                sp.wait_ge(x_stored[n], stored)
                for j in (3, 0, 1, 2):
                    for t in range(2):
                        rows = x_dram[n][K * t + 16 * j:K * t + 16 * j + 16]
                        sp.dma_start(x_forms[n][:, t, j],
                                     rows.unsqueeze(0).broadcast_to([8, 16, C])).then_inc(x_loaded[n], 16)

            def x0_reread(x0_read, h_read):
                sp.wait_ge(x0_loaded, x0_read)
                sp.wait_ge(h_loaded, h_read)

            sp.dma_start(ids_all[:], ids).then_inc(ids_loaded, 16)
            sp.dma_start(table_base[:], base).then_inc(ids_loaded, 16)
            gathered = 16 * 2 * G
            read_x0, read_h = 16 * 2 * NI, 16 * 2 * NH
            store_x0(gathered, gathered_rows[1])
            load_x0(32, 0)

            store_x(0, 1)
            load_x(0, 16)
            x0_reread(read_x0, read_h)
            store_x0(2 * gathered, gathered_rows[0])
            sp.wait_ge(z_vector_ready, UNITS)
            load_x0(2 * 32, 1)

            store_x(1, 1)
            store_x(0, 2)
            sp.wait_ge(z_vector_ready, 3 * UNITS)
            sp.wait_ge(z_pool_ready, UNITS)
            load_x(0, 2 * 16)
            x0_reread(2 * read_x0, 2 * read_h)
            store_x0(3 * gathered, gathered_rows[0])
            load_x0(3 * 32, 2)
            load_x(1, 16)
            x0_reread(3 * read_x0, 3 * read_h)
            store_x0(4 * gathered, gathered_rows[0])

            def step(p, load_next=True, store_second_next=True):
                held = (lambda x: x) if isinstance(p, int) else (lambda x: sp.snap(sp.to_reg(x)))
                slot = held((p + 1) % SLOTS)
                this, next_ = held(p), held(p + 1)
                vector_before, pool_before = held(vector_units_before(p)), held(pool_units_before(p))
                vector_layer_2 = held(vector_units_before(p) + 2 * UNITS)
                pool_layer_2 = held(pool_units_before(p) + UNITS)
                x2_reread, x2_there, x1_there = held(16 * 2 * NJ * (p - 1)), held(16 * p), held(16 * (p + 1))
                x0_there = held(32 * (p + 2))
                x0_read, h_read = held(16 * 2 * NI * (p + 2)), held(16 * 2 * NH * (p + 2))
                rows_there = held(16 * 2 * G * (p + 3))

                sp.wait_ge(x_loaded[1], x2_reread)
                store_x(1, this)
                store_x(0, next_)
                sp.wait_ge(z_vector_ready, vector_before)
                sp.wait_ge(z_pool_ready, pool_before)
                load_x(0, x1_there)
                sp.wait_ge(z_vector_ready, vector_layer_2)
                sp.wait_ge(z_pool_ready, pool_layer_2)
                if load_next:
                    load_x0(x0_there, slot)
                load_x(1, x2_there)
                if load_next:
                    x0_reread(x0_read, h_read)
                if store_second_next:
                    store_x0(rows_there, gathered_rows[0])

            with sp.Fori(2, NP - 2) as p:
                step(p)
            step(NP - 2, store_second_next=False)
            step(NP - 1, load_next=False, store_second_next=False)

            sp.wait_ge(x_loaded[1], 16 * 2 * NJ * (NP - 1))
            store_x(1, NP)
            sp.wait_ge(z_vector_ready, vector_units_before(NP) + UNITS)
            sp.wait_ge(z_pool_ready, pool_units_before(NP) + UNITS)
            load_x(1, 16 * NP)

            sp.wait_ge(y_ready, 1)
            for t in range(2):
                sp.dma_start(out.rearrange("(p t b) o -> t o p b", t=2, b=TB)[t],
                             y_sb[0:1, t * (B // 2):(t + 1) * (B // 2)].rearrange("o (p b) -> o p b", b=TB)
                             ).then_inc(y_stored, 16)
            sp.wait_ge(y_stored, 32)

        @block.gpsimd
        def _(pool):
            def new_index(p):
                if not (isinstance(p, int) and p == 0):
                    pool.wait_ge(rows_gathered, 16 * 2 * G * p)
                nc.gpsimd.tensor_tensor(row_index[:], ids_all[:, p], table_base[:], ALU.add
                                        ).then_inc(index_ready, 1)
                if not (isinstance(p, int) and p < 2):
                    pool.wait_ge(x0_stored, 32 * p)
                pool.wait_ge(index_ready, p + 1)
                pool.sem_inc(gathers_begun, 1)

            def gather(p, t, rows):
                for g in range(G):
                    at = t * G + g
                    nc.gpsimd.indirect_dma_start(
                        rows[:, t, g], None, table,
                        bass.IndirectOffsetOnAxis(ap=row_index[:, at:at + 1], axis=0)
                    ).then_inc(rows_gathered, 16)

            def products(n, p, slot, before, first=False):
                pool.wait_ge(x_loaded[n], 16 * 2 * NJ * (p + 1))
                for u in range(UNITS):
                    half, t = divmod(u, 2)
                    if not first:
                        pool.wait_ge(z_pool_used, before + u - UNITS + 1)
                    nc.gpsimd.tensor_tensor(
                        z_pool[:, u],
                        x0_forms[:, slot, t, 2 * half:2 * half + 2],
                        x_forms[n][:, t, NJ - 1].unsqueeze(1).broadcast_to([128, 2, C]),
                        ALU.mult).then_inc(z_pool_ready, 1)

            pool.wait_ge(ids_loaded, 32)
            new_index(0)
            gather(0, 0, gathered_rows[1])
            gather(0, 1, gathered_rows[1])
            new_index(1)
            gather(1, 0, gathered_rows[0])
            gather(1, 1, gathered_rows[0])
            for p in range(2):
                pool.wait_ge(x0_loaded, 16 * 2 * NI * (p + 1))
                products(0, p, p, UNITS * p, first=p == 0)
                new_index(p + 2)
                gather(p + 2, 0, gathered_rows[0])
                gather(p + 2, 1, gathered_rows[0])

            def step(p, slot, last_slot, gather_second_next=True):
                if gather_second_next:
                    new_index(p + 2)
                    gather(p + 2, 0, gathered_rows[0])
                products(1, p - 2, last_slot, pool_units_before(p))
                if gather_second_next:
                    gather(p + 2, 1, gathered_rows[0])
                products(0, p, slot, pool_units_before(p) + UNITS)

            with pool.Fori(2, NP - 2) as p:
                step(p, pool.snap(p % SLOTS), pool.snap((p - 2) % SLOTS))
            for p in (NP - 2, NP - 1):
                step(p, p % SLOTS, (p - 2) % SLOTS, gather_second_next=False)
            for n in range(2):
                products(1, NP - 2 + n, (NP - 2 + n) % SLOTS, pool_units_before(NP) + n * UNITS)

        @block.scalar
        def _(act):
            def relu(n, p, units):
                act.wait_ge(z_vector_used if n == 0 else z_pool_used, units)
                act.wait_ge(x_summed[n], p + COUNT_0[n])
                if n < 2:
                    act.wait_ge(x_stored[n], 16 * p)
                nc.scalar.activation(x_sb[n][:], result[n][:], ACT.Relu).then_inc(x_ready[n], 1)

            def copies(slot, before, relu_between=None, first=False):
                for u in range(UNITS):
                    half, t = divmod(u, 2)
                    if not (first and u < 2):
                        act.wait_ge(z_vector_ready, before + u - 1)
                    nc.scalar.activation(x0_psum[:, t], x0_forms[:, slot, t, 2 * half:2 * half + 2],
                                         ACT.Copy).then_inc(x0_copied, 1)
                    if u == 2 and relu_between:
                        relu(*relu_between)

            act.sem_inc(x_ready[2], COUNT_0[2])
            act.dma_start(w0_plain[:], w0).then_inc(w0_loaded, 16)
            act.dma_start(w0_extra[:], w0_mirror).then_inc(w0_loaded, 16)
            act.dma_start(w12_sb[:], w12).then_inc(w12_loaded, 16)
            for t in range(2):
                rows = slice(K * t, K * t + K)
                act.dma_start(w_top1_sb[rows],
                              w_top1[0:3 * K].rearrange("(l k) n -> k l n", k=K)).then_inc(top_loaded, 16)
                act.dma_start(w_dense_sb[K * t:K * t + D], w_top1[3 * K:3 * K + D]).then_inc(top_loaded, 16)
                act.dma_start(dense_sb[K * t:K * t + D], dense[t]).then_inc(top_loaded, 16)
            act.dma_start(w_top2_sb[:], w_top2).then_inc(top_loaded, 16)
            act.dma_start(w_top3_sb[:], w_top3).then_inc(top_loaded, 16)
            act.dma_start(b_top1_sb[:], b_top1).then_inc(top_loaded, 16)
            act.dma_start(b_top2_sb[:], b_top2).then_inc(top_loaded, 16)

            for p in range(2):
                act.wait_ge(x0_loaded, 16 * 2 * NI * (p + 1))
                if p == 0:
                    copies(0, 0, first=True)
                else:
                    copies(p, 2 * UNITS, relu_between=(1, 0, UNITS))
                relu(0, p, (2 * p + 1) * UNITS)
                copies(p, (2 * p + 1) * UNITS)

            with act.Fori(2, NP, SLOTS) as first:
                for k in range(SLOTS):
                    p, slot = first + k, (2 + k) % SLOTS
                    before, pool_before = vector_units_before(p), pool_units_before(p)
                    act.wait_ge(x0_loaded, 16 * 2 * NI * (p + 1))
                    copies(slot, before, relu_between=(1, p - 1, pool_before))
                    copies((slot - 2) % SLOTS, before + UNITS, relu_between=(0, p, before + UNITS))
                    copies(slot, before + 2 * UNITS, relu_between=(2, p - 2, pool_before + UNITS))
            for n, (layer, p) in enumerate(((1, NP - 1), (2, NP - 2))):
                copies((NP - 2 + n) % SLOTS, vector_units_before(NP) + n * UNITS,
                       relu_between=(layer, p, pool_units_before(NP) + n * UNITS))
            relu(2, NP - 1, pool_units_before(NP) + 2 * UNITS)

            act.wait_ge(top_loaded, 16 * 10)
            act.wait_ge(hidden1_summed, 1)
            for n in range(N1):
                nc.scalar.activation(hidden1[:, n].rearrange("p (t c) -> p t c", t=2), top1_psum[:, :, n],
                                     ACT.Relu, bias=b_top1_sb[:, n:n + 1]).then_inc(hidden1_ready, 1)
            for n in range(N2):
                act.wait_ge(hidden2_summed, n + 1)
                nc.scalar.activation(hidden2[:, n], result[n][:], ACT.Relu,
                                     bias=b_top2_sb[:, n:n + 1]).then_inc(hidden2_ready, 1)
            act.wait_ge(y_summed, 1)
            nc.scalar.activation(y_sb[:], y_psum[0:1], ACT.Copy).then_inc(y_ready, 1)

        @block.vector
        def _(dve):
            def sum_d(n, p):
                dve.wait_ge(x_ready[n], p + 1 + COUNT_0[n])
                nc.vector.tensor_reduce(d_sums[:, n, bass.ds(p * TB, TB)],
                                        x_sb[n][:].rearrange("p (b d) -> p b d", d=D),
                                        AXIS.X, ALU.add).then_inc(x_summed[n], 1)

            def unit(z, left, right, u, before, first):
                dve.wait_ge(x0_copied, before + u + 1)
                if not first:
                    dve.wait_ge(z_vector_used, before + u - UNITS + 1)
                nc.vector.tensor_tensor(z, left, right, ALU.mult).then_inc(z_vector_ready, 1)

            def layer_0(p, before, first=False):
                dve.wait_ge(h_loaded, 16 * 2 * NH * (p + 1))
                for u in range(UNITS):
                    half, t = divmod(u, 2)
                    if half == 0:
                        unit(z_vector[:, u, 0:4].rearrange("p (j i) c -> p j i c", i=2),
                             x0_psum[:, t].unsqueeze(1).broadcast_to([128, NH, 2, C]),
                             h_forms[:, t].unsqueeze(2).broadcast_to([128, NH, 2, C]), u, before, first)
                    else:
                        unit(z_vector[:, u, 0:2], x0_psum[:, t],
                             h_forms[:, t, 1].unsqueeze(1).broadcast_to([128, 2, C]), u, before, first)

            def layer(n, p, before):
                dve.wait_ge(x_loaded[n], 16 * 2 * NJ * (p + 1))
                for u in range(UNITS):
                    t = u % 2
                    unit(z_vector[:, u].rearrange("p (j i) c -> p j i c", i=2),
                         x0_psum[:, t].unsqueeze(1).broadcast_to([128, JV, 2, C]),
                         x_forms[n][:, t, 0:JV].unsqueeze(2).broadcast_to([128, JV, 2, C]), u, before, False)

            dve.sem_inc(x_summed[2], COUNT_0[2])
            dve.wait_ge(w0_loaded, 32)
            nc.vector.tensor_tensor(w0_plain[:, 2:4], w0_plain[:, 2:4], w0_extra[:], ALU.add
                                    ).then_inc(w0_folded, 1)
            layer_0(0, 0, first=True)
            layer(0, 0, UNITS)
            sum_d(0, 0)
            layer_0(1, 2 * UNITS)
            sum_d(1, 0)
            layer(0, 1, 3 * UNITS)
            sum_d(0, 1)
            with dve.Fori(2, NP) as p:
                before = vector_units_before(p)
                layer_0(p, before)
                sum_d(1, p - 1)
                layer(1, p - 2, before + UNITS)
                sum_d(0, p)
                layer(0, p, before + 2 * UNITS)
                sum_d(2, p - 2)
            layer(1, NP - 2, vector_units_before(NP))
            sum_d(1, NP - 1)
            layer(1, NP - 1, vector_units_before(NP) + UNITS)
            sum_d(2, NP - 2)
            sum_d(2, NP - 1)

        @block.tensor
        def _(pe):
            def side_by_side(n, weights, z, u, first, last):
                for t in range(2):
                    done = nc.tensor.matmul(result[n][K * t:K * t + K], weights, z[:, u + t],
                                            start=first, stop=last)
                return done

            def layer_0(p, before):
                if not (isinstance(p, int) and p == 0):
                    pe.wait_ge(x_ready[0], p)
                for half in range(2):
                    pe.wait_ge(z_vector_ready, before + 2 * half + 2)
                    count = 4 if half == 0 else 2
                    for c in range(count):
                        done = side_by_side(0, w0_plain[:, 4 * half + c], z_vector[:, :, c], 2 * half,
                                            half == 0 and c == 0, half == 1 and c == count - 1)
                    done.then_inc(z_vector_used, 2)

            def layer(n, p, before, pool_before):
                if not (isinstance(p, int) and p == 0):
                    pe.wait_ge(x_ready[n + 1], p + COUNT_0[n + 1])
                for half in range(2):
                    pe.wait_ge(z_vector_ready, before + 2 * half + 2)
                    for c in range(JV * 2):
                        done = side_by_side(n + 1, w12_sb[:, n, c // 2, 2 * half + c % 2],
                                            z_vector[:, :, c], 2 * half, half == 0 and c == 0, False)
                    done.then_inc(z_vector_used, 2)
                for half in range(2):
                    pe.wait_ge(z_pool_ready, pool_before + 2 * half + 2)
                    for c in range(2):
                        done = side_by_side(n + 1, w12_sb[:, n, NJ - 1, 2 * half + c],
                                            z_pool[:, :, c], 2 * half, False, half == 1 and c == 1)
                    done.then_inc(z_pool_used, 2)

            pe.wait_ge(w0_loaded, 32)
            pe.wait_ge(w0_folded, 1)
            layer_0(0, 0)
            pe.wait_ge(w12_loaded, 16)
            layer(0, 0, UNITS, 0)
            layer_0(1, 2 * UNITS)
            layer(0, 1, 3 * UNITS, UNITS)
            with pe.Fori(2, NP) as p:
                before, pool_before = vector_units_before(p), pool_units_before(p)
                layer_0(p, before)
                layer(1, p - 2, before + UNITS, pool_before)
                layer(0, p, before + 2 * UNITS, pool_before + UNITS)
            for n in range(2):
                layer(1, NP - 2 + n, vector_units_before(NP) + n * UNITS, pool_units_before(NP) + n * UNITS)

            pe.wait_ge(top_loaded, 16 * 10)
            for n in range(3):
                pe.wait_ge(x_summed[n], NP + COUNT_0[n])
            for m in range(N1):
                cols = slice(128 * m, 128 * m + 128)
                for n in range(3):
                    for t in range(2):
                        rows = slice(K * t, K * t + K)
                        nc.tensor.matmul(top1_psum[:, t, m], w_top1_sb[rows, n, cols], d_sums[rows, n],
                                         start=n == 0, stop=False)
                for t in range(2):
                    rows = slice(K * t, K * t + D)
                    done = nc.tensor.matmul(top1_psum[:, t, m], w_dense_sb[rows, cols], dense_sb[rows],
                                            start=False, stop=True)
            done.then_inc(hidden1_summed, 1)
            pe.wait_ge(x_ready[0], NP)
            pe.wait_ge(x_ready[1], NP)
            for m in range(N2):
                for n in range(N1):
                    pe.wait_ge(hidden1_ready, n + 1)
                    done = nc.tensor.matmul(result[m][:], w_top2_sb[:, n, 128 * m:128 * m + 128],
                                            hidden1[:, n], start=n == 0, stop=n == N1 - 1)
                done.then_inc(hidden2_summed, 1)
            for n in range(N2):
                pe.wait_ge(hidden2_ready, n + 1)
                done = nc.tensor.matmul(y_psum[0:1], w_top3_sb[:, n:n + 1], hidden2[:, n],
                                        start=n == 0, stop=n == N2 - 1)
            done.then_inc(y_summed, 1)


def kernel(**inputs):
    import concourse.bacc as bacc
    from concourse.bass_utils import run_bass_kernel_spmd

    a = {name: np.asarray(x) for name, x in inputs.items()}
    tables = [a[f"tbl_{m}"] for m in range(M)]
    starts = np.cumsum([0] + [t.shape[0] for t in tables[:-1]]).astype(np.int32)
    base = np.tile(np.repeat(starts.reshape(G, 4).T, TB, axis=0), (1, 2))
    ids = a["ids"].reshape(NP, 2, TB, G, 4).transpose(4, 2, 0, 1, 3).reshape(128, NP, 2 * G)

    def chunks(w, nj):
        return w.reshape(NI, 8, nj, 16, K).transpose(1, 3, 2, 0, 4).reshape(128, nj, NI, K)

    w0 = a["L0_rec_W0"]
    plain, mirror = chunks(w0, NH), chunks(w0.transpose(1, 0, 2), NH)
    w0_used = np.concatenate([plain[:, 0, 0:2], plain[:, 1, 0:2], plain[:, 1, 2:4]], axis=1)
    w12 = np.stack([chunks(a["L0_rec_W1"], NJ), chunks(a["L0_rec_W2"], NJ)], axis=1)
    dense = a["dense_ctx"].reshape(NP, 2, TB, D).transpose(1, 3, 0, 2).reshape(2, D, NP * TB)
    arrays = {
        "table": np.concatenate(tables, axis=0), "ids": ids, "base": base,
        "w0": w0_used, "w0_mirror": mirror[:, 1, 0:2], "w12": w12, "dense": dense,
        "w_top1": a["W_top1"], "b_top1": a["b_top1"].reshape(N1, 128).T,
        "w_top2": a["W_top2"].reshape(N1, 128, H2).transpose(1, 0, 2),
        "b_top2": a["b_top2"].reshape(N2, 128).T,
        "w_top3": a["W_top3"].reshape(N2, 128).T,
    }
    arrays = {name: np.ascontiguousarray(x) for name, x in arrays.items()}

    nc = bacc.Bacc("TRN2", target_bir_lowering=False, num_devices=1)
    ins = [nc.dram_tensor(name, x.shape, mybir.dt.from_np(x.dtype), kind="ExternalInput").ap()
           for name, x in arrays.items()]
    out = nc.dram_tensor("y", (B, 1), F32, kind="ExternalOutput").ap()
    build(nc, *ins, out)
    return run_bass_kernel_spmd(nc, [arrays], core_ids=[0]).results[0]["y"]
```

```python
from contextlib import ExitStack

import numpy as np

import concourse.bass as bass
from concourse import mybir

F32 = mybir.dt.float32
I32 = mybir.dt.int32
ALU = mybir.AluOpType
ACT = mybir.ActivationFunctionType
AXIS = mybir.AxisListType

B, M, D, K = 512, 32, 16, 64
TB = 32
C = TB * D
NP = B // (2 * TB)
NI, NJ = M // 8, K // 16
JV = NJ - 1
NH = M // 16
G = M // 4
UNITS = 4
RING = 5
FIRST = 4
SLOTS = 3
H1, H2 = 512, 256
N1, N2 = H1 // 128, H2 // 128
EARLY = NP - 2
LATE = (NP - EARLY) * 2 * TB


COUNT_0 = (0, 0, 1)


def vector_units_before(p):
    return 3 * UNITS * p - 2 * UNITS


def slots_before(p):
    return (2 + 2 * UNITS) * p - 2 * UNITS


def ring_slot(k):
    return k % RING


def pool_units_before(p):
    return 2 * UNITS * p - 2 * UNITS


def build(nc, table, ids, base, w0, w0_mirror, w12, dense, w_top1, b_top1, w_top2, b_top2, w_top3, out):
    x0_dram = nc.dram_tensor("x0_rows", (2, M, C), F32).ap()
    x_dram = [nc.dram_tensor(f"x{n + 1}_rows", (2 * K, C), F32).ap() for n in range(2)]

    with ExitStack() as ctx:
        def sb(name, shape, dt=F32):
            return ctx.enter_context(nc.sbuf_tensor(name, shape, dt))

        def sem(name):
            return ctx.enter_context(nc.semaphore(name))

        ids_all = sb("ids_all", [128, NP, 2 * G], I32)
        table_base = sb("table_base", [128, 2 * G], I32)
        first_index = sb("first_index", [128, FIRST, 2 * G], I32)
        row_index = sb("row_index", [128, 2 * G], I32)
        gathered_rows = [sb(f"gathered_rows{n}", [128, 2, G, D]) for n in range(2)]
        x0_forms = sb("x0_forms", [128, SLOTS, 2, NI, C])
        h_forms = sb("h_forms", [128, 2, NH, C])
        x_forms = [sb(f"x{n + 1}_forms", [128, 2, NJ, C]) for n in range(2)]
        z_vector = sb("z_vector", [128, RING, JV * 2, C])
        z_pool = sb("z_pool", [128, UNITS, 2, C])
        w0_plain = sb("w0_plain", [128, 6, K])
        w0_extra = sb("w0_extra", [128, 2, K])
        w12_sb = sb("w12_sb", [128, 2, NJ, NI, K])
        x_sb = [sb(f"x{n + 1}_sb", [128, C]) for n in range(3)]
        d_sums = sb("d_sums", [128, 3, NP * TB])
        top_in = sb("top_in", [128, 2, 2, NP * TB])
        w_top1_sb = sb("w_top1_sb", [128, 2, H1])
        w_top2_sb = sb("w_top2_sb", [128, N1, H2])
        w_top3_sb = sb("w_top3_sb", [128, N2])
        b_top1_sb = sb("b_top1_sb", [128, N1])
        b_top2_sb = sb("b_top2_sb", [128, N2])
        hidden1 = h_forms[:].rearrange("p t j c -> p (t j c)")[:, 0:N1 * EARLY * 2 * TB].rearrange(
            "p (k c) -> p k c", k=N1)
        hidden2 = sb("hidden2", [128, N2, EARLY * 2 * TB])
        late1 = sb("late1", [128, N1, LATE])
        late2 = sb("late2", [128, N2, LATE])
        y_sb = sb("y_sb", [1, 2, NP * TB])

        x0_psum = ctx.enter_context(nc.psum_tensor("x0_psum", [128, 2, 2, C], F32))
        result = [ctx.enter_context(nc.psum_tensor(f"result{n}", [128, C], F32)) for n in range(3)]
        y_psum = ctx.enter_context(nc.psum_tensor("y_psum", [128, B], F32))
        early_banks = [result[0], y_psum, result[1]]
        late1_psum = [x0_psum[:, t, 0].rearrange("p (k c) -> p k c", c=LATE) for t in range(2)]
        late2_psum = [x0_psum[:, t, 1] for t in range(2)]
        late3_psum = result[2]

        ids_loaded = sem("ids_loaded")
        w0_loaded = sem("w0_loaded")
        w12_loaded = sem("w12_loaded")
        top_loaded = sem("top_loaded")
        w0_folded = sem("w0_folded")
        index_ready = sem("index_ready")
        gathers_begun = sem("gathers_begun")
        rows_gathered = [[sem(f"rows_gathered_{which}_t{t}") for t in range(2)]
                         for which in ("even", "odd", "rest")]
        x0_stored = [sem(f"x0_stored_t{t}") for t in range(2)]
        x0_loaded = [sem(f"x0_loaded_t{t}") for t in range(2)]
        h_loaded = [sem(f"h_loaded_t{t}") for t in range(2)]
        x_stored = [sem(f"x{n + 1}_stored") for n in range(2)]
        x_loaded = [[sem(f"x{n + 1}_loaded_t{t}") for t in range(2)] for n in range(2)]
        x0_copied = sem("x0_copied")
        z_vector_ready = sem("z_vector_ready")
        z_vector_used = sem("z_vector_used")
        z_pool_ready = sem("z_pool_ready")
        z_pool_used = sem("z_pool_used")
        x_ready = [sem(f"x{n + 1}_ready") for n in range(3)]
        x_summed = [sem(f"x{n + 1}_summed") for n in range(3)]
        early_in_ready = sem("early_in_ready")
        early_summed = sem("early_summed")
        early_ready = sem("early_ready")
        late_in_ready = sem("late_in_ready")
        late1_summed = sem("late1_summed")
        late2_summed = sem("late2_summed")
        late3_summed = sem("late3_summed")
        late1_by_scalar = sem("late1_by_scalar")
        late1_by_vector = sem("late1_by_vector")
        late2_by_scalar = sem("late2_by_scalar")
        late2_by_vector = sem("late2_by_vector")
        y_ready = sem("y_ready")
        y_stored = sem("y_stored")

        block = ctx.enter_context(nc.Block())

        @block.sync
        def _(sp):
            def store_x0(which, gathered, rows):
                for t in range(2):
                    sp.wait_ge(rows_gathered[which][t], gathered)
                    sp.dma_start(x0_dram[t].rearrange("(g m) (b d) -> (m b) g d", m=4, d=D),
                                 rows[:, t]).then_inc(x0_stored[t], 16)

            def load_x0(pairs_16, slot, tiles=(0, 1)):
                for t in tiles:
                    sp.wait_ge(x0_stored[t], pairs_16)
                    sp.dma_start(h_forms[:, t].rearrange("p j c -> p (j c)"),
                                 x0_dram[t].rearrange("(h j) c -> h (j c)", j=NH)
                                 .unsqueeze(0).broadcast_to([8, 16, NH * C])).then_inc(h_loaded[t], 16)
                    sp.dma_start(x0_forms[:, slot, t].rearrange("p i c -> p (i c)"),
                                 x0_dram[t].rearrange("(m i) c -> m (i c)", i=NI)
                                 .unsqueeze(1).broadcast_to([8, 16, NI * C])).then_inc(x0_loaded[t], 16)

            def x0_reread(pairs_16):
                for t in range(2):
                    sp.wait_ge(x0_loaded[t], pairs_16)
                    sp.wait_ge(h_loaded[t], pairs_16)

            def store_x(n, pairs):
                sp.wait_ge(x_ready[n], pairs)
                sp.dma_start(x_dram[n], x_sb[n][:]).then_inc(x_stored[n], 16)

            def load_x(n, pairs_16, forms=None):
                forms = x_forms[n] if forms is None else forms
                sp.wait_ge(x_stored[n], pairs_16)
                for t in range(2):
                    sp.dma_start(forms[:, t].rearrange("p j c -> p (j c)"),
                                 x_dram[n][K * t:K * t + K].rearrange("(h j) c -> h (j c)", j=NJ)
                                 .unsqueeze(0).broadcast_to([8, 16, NJ * C])).then_inc(x_loaded[n][t], 16)

            def x_reread(n, pairs_16):
                for t in range(2):
                    sp.wait_ge(x_loaded[n][t], pairs_16)

            sp.dma_start(ids_all[:], ids).then_inc(ids_loaded, 16)
            gathered = 16 * G
            for t in range(2):
                sp.wait_ge(rows_gathered[0][t], gathered)
                sp.dma_start(x0_dram[t].rearrange("(g m) (b d) -> (m b) g d", m=4, d=D),
                             gathered_rows[1][:, t]).then_inc(x0_stored[t], 16)
                load_x0(16, 0, (t,))

            x0_reread(16)
            store_x0(1, gathered, gathered_rows[0])
            sp.wait_ge(z_vector_ready, UNITS)
            load_x0(2 * 16, 1)

            store_x(0, 1)
            load_x(0, 16, x_forms[1])
            x_reread(0, 16)
            store_x(0, 2)
            load_x(0, 2 * 16)

            x0_reread(2 * 16)
            store_x0(0, 2 * gathered, gathered_rows[1])
            sp.wait_ge(z_vector_ready, 2 * UNITS)
            load_x0(3 * 16, 2)
            x0_reread(3 * 16)
            store_x0(2, gathered, gathered_rows[0])

            store_x(1, 1)
            sp.wait_ge(z_vector_ready, 3 * UNITS)
            sp.wait_ge(z_pool_ready, UNITS)
            load_x(1, 16)

            def step(p, load_next=True, store_second_next=True):
                held = (lambda x: x) if isinstance(p, int) else (lambda x: sp.snap(sp.to_reg(x)))
                slot = held((p + 1) % SLOTS)
                this, next_ = held(p), held(p + 1)
                vector_before, pool_before = held(vector_units_before(p)), held(pool_units_before(p))
                vector_layer_2 = held(vector_units_before(p) + 2 * UNITS)
                pool_layer_2 = held(pool_units_before(p) + UNITS)
                p_16, p1_16, p2_16, last_16 = (held(16 * (p + k)) for k in (0, 1, 2, -1))
                rows_there = held(gathered * p)

                x_reread(0, p_16)
                store_x(0, next_)
                sp.wait_ge(z_vector_ready, vector_before)
                sp.wait_ge(z_pool_ready, pool_before)
                load_x(0, p1_16)
                x_reread(1, last_16)
                store_x(1, this)
                sp.wait_ge(z_vector_ready, vector_layer_2)
                sp.wait_ge(z_pool_ready, pool_layer_2)
                if load_next:
                    load_x0(p2_16, slot)
                load_x(1, p_16)
                if load_next:
                    x0_reread(p2_16)
                if store_second_next:
                    store_x0(2, rows_there, gathered_rows[0])

            with sp.Fori(2, NP - 2) as p:
                step(p)
            step(NP - 2, store_second_next=False)
            step(NP - 1, load_next=False, store_second_next=False)

            x_reread(1, 16 * (NP - 1))
            store_x(1, NP)
            sp.wait_ge(z_vector_ready, vector_units_before(NP) + UNITS)
            sp.wait_ge(z_pool_ready, pool_units_before(NP) + UNITS)
            load_x(1, 16 * NP)

            sp.wait_ge(y_ready, 2)
            for t in range(2):
                sp.dma_start(out.rearrange("(p t b) o -> t o p b", t=2, b=TB)[t],
                             y_sb[:, t].rearrange("o (p b) -> o p b", b=TB)
                             ).then_inc(y_stored, 16)
            sp.wait_ge(y_stored, 32)

        @block.gpsimd
        def _(pool):
            def new_index(p):
                for t in range(2):
                    pool.wait_ge(rows_gathered[2][t], 16 * G * (p - 3))
                nc.gpsimd.tensor_tensor(row_index[:], ids_all[:, p], table_base[:], ALU.add
                                        ).then_inc(index_ready, 1)
                for t in range(2):
                    pool.wait_ge(x0_stored[t], 16 * p)
                pool.wait_ge(index_ready, p - FIRST + 2)
                pool.sem_inc(gathers_begun, 1)

            def gather(t, rows, which=2, index=row_index):
                for g in range(G):
                    at = t * G + g
                    nc.gpsimd.indirect_dma_start(
                        rows[:, t, g], None, table,
                        bass.IndirectOffsetOnAxis(ap=index[:, at:at + 1], axis=0)
                    ).then_inc(rows_gathered[which][t], 16)

            def products(n, p, slot, before, first=False, forms=None):
                forms = x_forms[n] if forms is None else forms
                for u in range(UNITS):
                    half, t = divmod(u, 2)
                    if half == 0:
                        pool.wait_ge(x_loaded[n][t], 16 * (p + 1))
                    if not first:
                        pool.wait_ge(z_pool_used, before + u - UNITS + 1)
                    nc.gpsimd.tensor_tensor(
                        z_pool[:, u],
                        x0_forms[:, slot, t, half::2],
                        forms[:, t, NJ - 1].unsqueeze(1).broadcast_to([128, 2, C]),
                        ALU.mult).then_inc(z_pool_ready, 1)

            pool.wait_ge(ids_loaded, 32)
            nc.gpsimd.tensor_tensor(first_index[:], ids_all[:, 0:FIRST],
                                    table_base[:].unsqueeze(1).broadcast_to([128, FIRST, 2 * G]), ALU.add
                                    ).then_inc(index_ready, 1)
            pool.wait_ge(index_ready, 1)
            for p in range(FIRST):
                rows = gathered_rows[1 - p % 2]
                for t in range(2):
                    if p >= 2:
                        pool.wait_ge(x0_stored[t], 16 * (p - 1))
                    if p == 3 and t == 1:
                        for s in range(2):
                            pool.wait_ge(x0_loaded[s], 16)
                        products(0, 0, 0, 0, first=True, forms=x_forms[1])
                    gather(t, rows, (0, 1, 0, 2)[p], first_index[:, p])
            for t in range(2):
                pool.wait_ge(x0_loaded[t], 2 * 16)
            products(0, 1, 1, UNITS)

            def step(p, slot, last_slot, gather_second_next=True):
                if gather_second_next:
                    new_index(p + 2)
                    gather(0, gathered_rows[0])
                products(1, p - 2, last_slot, pool_units_before(p))
                if gather_second_next:
                    gather(1, gathered_rows[0])
                products(0, p, slot, pool_units_before(p) + UNITS)

            with pool.Fori(2, NP - 2) as p:
                step(p, pool.snap(p % SLOTS), pool.snap((p - 2) % SLOTS))
            for p in (NP - 2, NP - 1):
                step(p, p % SLOTS, (p - 2) % SLOTS, gather_second_next=False)
            for n in range(2):
                products(1, NP - 2 + n, (NP - 2 + n) % SLOTS, pool_units_before(NP) + n * UNITS)

        @block.scalar
        def _(act):
            def relu(n, p, consumed):
                act.wait_ge(z_vector_used if n == 0 else z_pool_used, consumed)
                act.wait_ge(x_summed[n], p + COUNT_0[n])
                if n < 2:
                    act.wait_ge(x_stored[n], 16 * p)
                nc.scalar.activation(x_sb[n][:], result[n][:], ACT.Relu).then_inc(x_ready[n], 1)

            def copies(slot, before, loaded=None, relus=(), first=False, between={}, relus_after=2):
                for u in range(UNITS):
                    half, t = divmod(u, 2)
                    if u < 2 and loaded is not None:
                        act.wait_ge(x0_loaded[t], loaded)
                    if not (first and u < 2):
                        act.wait_ge(z_vector_ready, before + u - 1)
                    nc.scalar.activation(x0_psum[:, t], x0_forms[:, slot, t, half::2],
                                         ACT.Copy).then_inc(x0_copied, 1)
                    if u == relus_after:
                        for r in relus:
                            relu(*r)
                    if u in between:
                        between[u]()

            act.dma_start(table_base[:], base).then_inc(ids_loaded, 16)
            act.sem_inc(x_ready[2], COUNT_0[2])
            act.dma_start(w0_plain[:], w0).then_inc(w0_loaded, 16)
            act.dma_start(w0_extra[:], w0_mirror).then_inc(w0_loaded, 16)
            act.dma_start(w12_sb[:], w12).then_inc(w12_loaded, 16)
            act.dma_start(w_top1_sb[:, 0], w_top1[0:128]).then_inc(top_loaded, 16)
            act.dma_start(w_top1_sb[0:K + D, 1], w_top1[128:128 + K + D]).then_inc(top_loaded, 16)
            act.dma_start(top_in[K:K + D, 1], dense).then_inc(top_loaded, 16)
            act.dma_start(w_top2_sb[:], w_top2).then_inc(top_loaded, 16)
            act.dma_start(w_top3_sb[:], w_top3).then_inc(top_loaded, 16)
            act.dma_start(b_top1_sb[:], b_top1).then_inc(top_loaded, 16)
            act.dma_start(b_top2_sb[:], b_top2).then_inc(top_loaded, 16)

            copies(0, 0, loaded=16, first=True)
            relu(0, 0, 2)
            copies(1, UNITS, loaded=2 * 16)
            copies(0, 2 * UNITS, relus=[(0, 1, 4)], relus_after=1)
            copies(1, 3 * UNITS, relus=[(1, 0, UNITS)], relus_after=1)

            with act.Fori(2, NP, SLOTS) as first:
                for k in range(SLOTS):
                    p, slot = first + k, (2 + k) % SLOTS
                    before, pool_before = vector_units_before(p), pool_units_before(p)
                    copies(slot, before, loaded=16 * (p + 1))
                    copies((slot - 2) % SLOTS, before + UNITS,
                           relus=[(0, p, slots_before(p) + 2), (1, p - 1, pool_before)])
                    copies(slot, before + 2 * UNITS, relus=[(2, p - 2, pool_before + UNITS)])

            def top_block(n, t, pairs, ready):
                nc.scalar.activation(top_in[K * (n % 2):K * (n % 2) + K, n // 2, t, TB * pairs[0]:TB * pairs[1]],
                                     d_sums[K * t:K * t + K, n, TB * pairs[0]:TB * pairs[1]],
                                     ACT.Copy).then_inc(ready, 1)

            def early_inputs():
                for n in range(3):
                    act.wait_ge(x_summed[n], EARLY + COUNT_0[n])
                    for t in range(2):
                        top_block(n, t, (0, EARLY), early_in_ready)

            def early(k):
                act.wait_ge(early_summed, k + 1)
                bank = early_banks[k % 3]
                if k < N1:
                    nc.scalar.activation(hidden1[:, k, 0:EARLY * 2 * TB], bank[:, 0:EARLY * 2 * TB], ACT.Relu,
                                         bias=b_top1_sb[:, k:k + 1]).then_inc(early_ready, 1)
                elif k < N1 + N2:
                    nc.scalar.activation(hidden2[:, k - N1, 0:EARLY * 2 * TB], bank[:, 0:EARLY * 2 * TB], ACT.Relu,
                                         bias=b_top2_sb[:, k - N1:k - N1 + 1]).then_inc(early_ready, 1)
                else:
                    nc.scalar.activation(y_sb[:, :, 0:EARLY * TB],
                                         bank[0:1, 0:EARLY * 2 * TB].rearrange("o (t c) -> o t c", t=2),
                                         ACT.Copy).then_inc(y_ready, 1)

            act.wait_ge(top_loaded, 16 * 7)
            before, pool_before = vector_units_before(NP), pool_units_before(NP)
            copies((NP - 2) % SLOTS, before, relus=[(1, NP - 1, pool_before)], between={1: early_inputs})
            copies((NP - 1) % SLOTS, before + UNITS, relus=[(2, NP - 2, pool_before + UNITS)],
                   between={0: lambda: early(0), 1: lambda: early(1)})
            for n in range(2):
                act.wait_ge(x_summed[n], NP)
                for t in range(2):
                    top_block(n, t, (EARLY, NP), late_in_ready)
            for k in range(2, N1 + 1):
                early(k)
            relu(2, NP - 1, pool_before + 2 * UNITS)
            for k in range(N1 + 1, N1 + N2 + 1):
                early(k)
            act.wait_ge(x_summed[2], NP + COUNT_0[2])
            top_block(2, 0, (EARLY, NP), late_in_ready)
            act.wait_ge(late1_summed, 1)
            for k in range(N1 // 2):
                nc.scalar.activation(late1[:, k], late1_psum[0][:, k], ACT.Relu,
                                     bias=b_top1_sb[:, k:k + 1]).then_inc(late1_by_scalar, 1)
            act.wait_ge(late2_summed, 1)
            nc.scalar.activation(late2[:, 0], late2_psum[0][:, 0:LATE], ACT.Relu,
                                 bias=b_top2_sb[:, 0:1]).then_inc(late2_by_scalar, 1)
            act.wait_ge(late3_summed, 1)
            nc.scalar.activation(y_sb[:, :, EARLY * TB:NP * TB],
                                 late3_psum[0:1, 0:LATE].rearrange("o (t c) -> o t c", t=2),
                                 ACT.Copy).then_inc(y_ready, 1)

        @block.vector
        def _(dve):
            def sum_d(n, p):
                dve.wait_ge(x_ready[n], p + 1 + COUNT_0[n])
                nc.vector.tensor_reduce(d_sums[:, n, bass.ds(p * TB, TB)],
                                        x_sb[n][:].rearrange("p (b d) -> p b d", d=D),
                                        AXIS.X, ALU.add).then_inc(x_summed[n], 1)

            def unit(z, left, right, copied, used):
                dve.wait_ge(x0_copied, copied)
                if used is not None:
                    dve.wait_ge(z_vector_used, used)
                nc.vector.tensor_tensor(z, left, right, ALU.mult).then_inc(z_vector_ready, 1)

            def layer_0(p, before, filled, start=0):
                for u in range(UNITS):
                    half, t = divmod(u, 2)
                    z = z_vector[:, ring_slot(start + t)]
                    if half == 0:
                        dve.wait_ge(h_loaded[t], 16 * (p + 1))
                        unit(z[:, 0:4].rearrange("p (j i) c -> p j i c", i=2),
                             x0_psum[:, t].unsqueeze(1).broadcast_to([128, NH, 2, C]),
                             h_forms[:, t].unsqueeze(2).broadcast_to([128, NH, 2, C]),
                             before + u + 1, must_be_used(filled, t))
                    else:
                        unit(z[:, 4:6], x0_psum[:, t],
                             h_forms[:, t, 1].unsqueeze(1).broadcast_to([128, 2, C]),
                             before + u + 1, None)

            def layer(n, p, before, filled, start, forms=None):
                forms = x_forms[n] if forms is None else forms
                for u in range(UNITS):
                    t = u % 2
                    if u < 2:
                        dve.wait_ge(x_loaded[n][t], 16 * (p + 1))
                    unit(z_vector[:, ring_slot(start + u)].rearrange("p (j i) c -> p j i c", i=2),
                         x0_psum[:, t].unsqueeze(1).broadcast_to([128, JV, 2, C]),
                         forms[:, t, 0:JV].unsqueeze(2).broadcast_to([128, JV, 2, C]),
                         before + u + 1, must_be_used(filled, u))

            def must_be_used(filled, k):
                if isinstance(filled, int) and filled + k < RING:
                    return None
                return filled + k - RING + 1

            dve.sem_inc(x_summed[2], COUNT_0[2])
            dve.wait_ge(w0_loaded, 32)
            nc.vector.tensor_tensor(w0_plain[:, 2:4], w0_plain[:, 2:4], w0_extra[:], ALU.add
                                    ).then_inc(w0_folded, 1)
            layer_0(0, 0, 0, -12)
            layer_0(1, UNITS, 2, -10)
            sum_d(0, 0)
            layer(0, 0, 2 * UNITS, 4, -8, forms=x_forms[1])
            sum_d(0, 1)
            layer(0, 1, 3 * UNITS, 8, -4)
            sum_d(1, 0)
            with dve.Fori(2, NP) as p:
                before, filled = vector_units_before(p), slots_before(p)
                layer_0(p, before, filled)
                layer(1, p - 2, before + UNITS, filled + 2, 2)
                sum_d(0, p)
                sum_d(1, p - 1)
                layer(0, p, before + 2 * UNITS, filled + 2 + UNITS, 2 + UNITS)
                sum_d(2, p - 2)
            layer(1, NP - 2, vector_units_before(NP), slots_before(NP), 0)
            sum_d(1, NP - 1)
            layer(1, NP - 1, vector_units_before(NP) + UNITS, slots_before(NP) + UNITS, UNITS)
            sum_d(2, NP - 2)
            sum_d(2, NP - 1)

            dve.wait_ge(x_summed[2], NP + COUNT_0[2])
            nc.vector.tensor_copy(top_in[0:K, 1, 1, TB * EARLY:TB * NP],
                                  d_sums[K:2 * K, 2, TB * EARLY:TB * NP]).then_inc(late_in_ready, 1)
            dve.wait_ge(late1_summed, 2)
            for k in range(N1 // 2, N1):
                nc.vector.tensor_scalar(late1[:, k], late1_psum[1][:, k - N1 // 2], b_top1_sb[:, k:k + 1], 0.0,
                                        ALU.add, ALU.max).then_inc(late1_by_vector, 1)
            dve.wait_ge(late2_summed, 2)
            nc.vector.tensor_scalar(late2[:, 1], late2_psum[1][:, 0:LATE], b_top2_sb[:, 1:2], 0.0,
                                    ALU.add, ALU.max).then_inc(late2_by_vector, 1)

        @block.tensor
        def _(pe):
            def side_by_side(n, weights, z, slots, first, last):
                for t in range(2):
                    done = nc.tensor.matmul(result[n][K * t:K * t + K], weights, z[:, slots[t]],
                                            start=first, stop=last)
                return done

            def layer_0(p, before, start=0):
                slots = ring_slot(start), ring_slot(start + 1)
                if not (isinstance(p, int) and p == 0):
                    pe.wait_ge(x_ready[0], p)
                for half in range(2):
                    pe.wait_ge(z_vector_ready, before + 2 * half + 2)
                    count = 4 if half == 0 else 2
                    for c in range(count):
                        done = side_by_side(0, w0_plain[:, 4 * half + c], z_vector[:, :, 4 * half + c],
                                            slots, half == 0 and c == 0, half == 1 and c == count - 1)
                done.then_inc(z_vector_used, 2)

            def layer(n, p, before, pool_before, start, between={}):
                if not (isinstance(p, int) and p == 0):
                    pe.wait_ge(x_ready[n + 1], p + COUNT_0[n + 1])
                for half in range(2):
                    slots = ring_slot(start + 2 * half), ring_slot(start + 2 * half + 1)
                    pe.wait_ge(z_vector_ready, before + 2 * half + 2)
                    for c in range(JV * 2):
                        done = side_by_side(n + 1, w12_sb[:, n, c // 2, half + 2 * (c % 2)],
                                            z_vector[:, :, c], slots, half == 0 and c == 0, False)
                    done.then_inc(z_vector_used, 2)
                    for k in between.get((half, "vector"), ()):
                        early(k)
                    pe.wait_ge(z_pool_ready, pool_before + 2 * half + 2)
                    for c in range(2):
                        done = side_by_side(n + 1, w12_sb[:, n, NJ - 1, half + 2 * c],
                                            z_pool[:, :, c], (2 * half, 2 * half + 1), False, half == 1 and c == 1)
                    done.then_inc(z_pool_used, 2)
                    for k in between.get((half, "pool"), ()):
                        early(k)

            def early(k):
                if k == 0:
                    pe.wait_ge(top_loaded, 16 * 7)
                    pe.wait_ge(early_in_ready, 6)
                if k == 2:
                    pe.wait_ge(x_ready[1], NP)
                if k >= 3:
                    pe.wait_ge(early_ready, k - 2)
                bank = early_banks[k % 3]
                if k < N1:
                    for half, rows in enumerate((128, K + D)):
                        done = nc.tensor.matmul(
                            bank[:, 0:EARLY * 2 * TB], w_top1_sb[0:rows, half, 128 * k:128 * k + 128],
                            top_in[0:rows, half, :, 0:EARLY * TB], start=half == 0, stop=half == 1)
                elif k < N1 + N2:
                    pe.wait_ge(early_ready, N1)
                    for n in range(N1):
                        done = nc.tensor.matmul(
                            bank[:, 0:EARLY * 2 * TB], w_top2_sb[:, n, 128 * (k - N1):128 * (k - N1) + 128],
                            hidden1[:, n], start=n == 0, stop=n == N1 - 1)
                else:
                    pe.wait_ge(early_ready, N1 + N2)
                    for n in range(N2):
                        done = nc.tensor.matmul(bank[0:1, 0:EARLY * 2 * TB], w_top3_sb[:, n:n + 1],
                                                hidden2[:, n], start=n == 0, stop=n == N2 - 1)
                done.then_inc(early_summed, 1)

            pe.wait_ge(w0_loaded, 32)
            pe.wait_ge(w0_folded, 1)
            layer_0(0, 0, -12)
            layer_0(1, UNITS, -10)
            pe.wait_ge(w12_loaded, 16)
            layer(0, 0, 2 * UNITS, 0, -8)
            layer(0, 1, 3 * UNITS, UNITS, -4)
            with pe.Fori(2, NP) as p:
                before, pool_before = vector_units_before(p), pool_units_before(p)
                layer_0(p, before)
                layer(1, p - 2, before + UNITS, pool_before, 2)
                layer(0, p, before + 2 * UNITS, pool_before + UNITS, 2 + UNITS)
            before, pool_before = vector_units_before(NP), pool_units_before(NP)
            layer(1, NP - 2, before, pool_before, 0, {(0, "vector"): [0], (0, "pool"): [1]})
            layer(1, NP - 1, before + UNITS, pool_before + UNITS, UNITS,
                  {(0, "vector"): [2], (0, "pool"): [3], (1, "vector"): [N1]})
            for k in range(N1 + 1, N1 + N2 + 1):
                early(k)

            pe.wait_ge(late_in_ready, 6)
            pe.wait_ge(z_vector_ready, before + 2 * UNITS)
            for k in range(N1):
                for half, rows in enumerate((128, K + D)):
                    done = nc.tensor.matmul(
                        late1_psum[k // 2][:, k % 2], w_top1_sb[0:rows, half, 128 * k:128 * k + 128],
                        top_in[0:rows, half, :, EARLY * TB:NP * TB], start=half == 0, stop=half == 1)
                if k % 2:
                    done.then_inc(late1_summed, 1)
            for m in range(N2):
                for k in range(N1):
                    if k < N1 // 2:
                        pe.wait_ge(late1_by_scalar, k + 1)
                    else:
                        pe.wait_ge(late1_by_vector, k - N1 // 2 + 1)
                    done = nc.tensor.matmul(late2_psum[m][:, 0:LATE], w_top2_sb[:, k, 128 * m:128 * m + 128],
                                            late1[:, k], start=k == 0, stop=k == N1 - 1)
                done.then_inc(late2_summed, 1)
            pe.wait_ge(late2_by_scalar, 1)
            nc.tensor.matmul(late3_psum[0:1, 0:LATE], w_top3_sb[:, 0:1], late2[:, 0], start=True, stop=False)
            pe.wait_ge(late2_by_vector, 1)
            nc.tensor.matmul(late3_psum[0:1, 0:LATE], w_top3_sb[:, 1:2], late2[:, 1],
                             start=False, stop=True).then_inc(late3_summed, 1)


def kernel(**inputs):
    import concourse.bacc as bacc
    from concourse.bass_utils import run_bass_kernel_spmd

    a = {name: np.asarray(x) for name, x in inputs.items()}
    tables = [a[f"tbl_{m}"] for m in range(M)]
    starts = np.cumsum([0] + [t.shape[0] for t in tables[:-1]]).astype(np.int32)
    base = np.tile(np.repeat(starts.reshape(G, 4).T, TB, axis=0), (1, 2))
    ids = a["ids"].reshape(NP, 2, TB, G, 4).transpose(4, 2, 0, 1, 3).reshape(128, NP, 2 * G)

    def chunks(w, nj):
        return w.reshape(8, NI, 16, nj, K).transpose(0, 2, 3, 1, 4).reshape(128, nj, NI, K)

    w0 = a["L0_rec_W0"]
    plain, mirror = chunks(w0, NH), chunks(w0.transpose(1, 0, 2), NH)
    w0_used = np.concatenate([plain[:, 0, 0::2], plain[:, 1, 0::2], plain[:, 1, 1::2]], axis=1)
    w12 = np.stack([chunks(a["L0_rec_W1"], NJ), chunks(a["L0_rec_W2"], NJ)], axis=1)
    dense = a["dense_ctx"].reshape(NP, 2, TB, D).transpose(3, 1, 0, 2).reshape(D, 2, NP * TB)
    arrays = {
        "table": np.concatenate(tables, axis=0), "ids": ids, "base": base,
        "w0": w0_used, "w0_mirror": mirror[:, 1, 0::2], "w12": w12, "dense": dense,
        "w_top1": a["W_top1"], "b_top1": a["b_top1"].reshape(N1, 128).T,
        "w_top2": a["W_top2"].reshape(N1, 128, H2).transpose(1, 0, 2),
        "b_top2": a["b_top2"].reshape(N2, 128).T,
        "w_top3": a["W_top3"].reshape(N2, 128).T,
    }
    arrays = {name: np.ascontiguousarray(x) for name, x in arrays.items()}

    nc = bacc.Bacc("TRN2", target_bir_lowering=False, num_devices=1)
    ins = [nc.dram_tensor(name, x.shape, mybir.dt.from_np(x.dtype), kind="ExternalInput").ap()
           for name, x in arrays.items()]
    out = nc.dram_tensor("y", (B, 1), F32, kind="ExternalOutput").ap()
    build(nc, *ins, out)
    return run_bass_kernel_spmd(nc, [arrays], core_ids=[0]).results[0]["y"]
```

```python
from contextlib import ExitStack

import numpy as np

import concourse.bass as bass
from concourse import mybir

F32 = mybir.dt.float32
I32 = mybir.dt.int32
ALU = mybir.AluOpType
ACT = mybir.ActivationFunctionType
AXIS = mybir.AxisListType

B, M, D, K = 512, 32, 16, 64
TB = 32
C = TB * D
NP = B // (2 * TB)
NI, NJ = M // 8, K // 16
JV = NJ - 1
NH = M // 16
CH0 = (3, 2)
MIXED = 16 * 4
G = M // 4
UNITS = 4
RING = 5
SLOTS = 3
H1, H2 = 512, 256
N1, N2 = H1 // 128, H2 // 128
EARLY = NP - 2
LATE = (NP - EARLY) * 2 * TB


COUNT_0 = (0, 0, 1)


def vector_units_before(p):
    return 3 * UNITS * p - 2 * UNITS


def slots_before(p):
    return (2 + 2 * UNITS) * p - 2 * UNITS


def ring_slot(k):
    return k % RING


def starts_before(p):
    return 2 * p - 2


def pool_units_before(p):
    return 2 * UNITS * p - 2 * UNITS


def build(nc, table, ids, base, odd_h16, w0, w0_mirror, w12, dense, w_top1, b_top1, w_top2, b_top2, w_top3, out):
    x0_dram = nc.dram_tensor("x0_rows", (2, 2, M, C), F32).ap()
    x_dram = [nc.dram_tensor(f"x{n + 1}_rows", (2 * K, C), F32).ap() for n in range(2)]

    with ExitStack() as ctx:
        def sb(name, shape, dt=F32):
            return ctx.enter_context(nc.sbuf_tensor(name, shape, dt))

        def sem(name):
            return ctx.enter_context(nc.semaphore(name))

        ids_all = sb("ids_all", [128, NP, 2 * G], I32)
        table_base = sb("table_base", [128, 2 * G], I32)
        row_index = [sb(f"row_index{n}", [128, 2 * G], I32) for n in range(2)]
        gathered_rows = [sb(f"gathered_rows{n}", [128, 2, G, D]) for n in range(2)]
        x0_forms = sb("x0_forms", [128, SLOTS, 2, NI, C])
        h_forms = sb("h_forms", [128, 2, NH + 1, C])
        x0_mixed = sb("x0_mixed", [128, 2, C])
        x_forms = [sb(f"x{n + 1}_forms", [128, 2, NJ, C]) for n in range(2)]
        z_vector = sb("z_vector", [128, RING, JV * 2, C])
        z_pool = sb("z_pool", [128, UNITS, 2, C])
        w0_plain = sb("w0_plain", [128, 5, K])
        w0_extra = sb("w0_extra", [128, 4, K])
        fold_odd = sb("fold_odd", [128, 1])
        w12_sb = sb("w12_sb", [128, 2, NJ, NI, K])
        x_sb = [sb(f"x{n + 1}_sb", [128, C]) for n in range(3)]
        d_sums = sb("d_sums", [128, 3, NP * TB])
        top_in = sb("top_in", [128, 2, 2, NP * TB])
        w_top1_sb = sb("w_top1_sb", [128, 2, H1])
        w_top2_sb = sb("w_top2_sb", [128, N1, H2])
        w_top3_sb = sb("w_top3_sb", [128, N2])
        b_top1_sb = sb("b_top1_sb", [128, N1])
        b_top2_sb = sb("b_top2_sb", [128, N2])
        hidden_at = [0]

        def hidden(blocks, columns):
            at = hidden_at[0]
            hidden_at[0] += blocks * columns
            return h_forms[:].rearrange("p t j c -> p (t j c)")[:, at:at + blocks * columns].rearrange(
                "p (k c) -> p k c", k=blocks)

        hidden1, hidden2 = hidden(N1, EARLY * 2 * TB), hidden(N2, EARLY * 2 * TB)
        late1, late2 = hidden(N1, LATE), hidden(N2, LATE)
        y_sb = x0_mixed[0:1, 0]

        x0_psum = ctx.enter_context(nc.psum_tensor("x0_psum", [128, 2, 2, C], F32))
        result = [ctx.enter_context(nc.psum_tensor(f"result{n}", [128, C], F32)) for n in range(3)]
        y_psum = ctx.enter_context(nc.psum_tensor("y_psum", [128, B], F32))
        early_banks = [result[0], y_psum, result[1]]
        late1_psum = [x0_psum[:, t, 0].rearrange("p (k c) -> p k c", c=LATE) for t in range(2)]
        late2_psum = [x0_psum[:, t, 1] for t in range(2)]
        late3_psum = result[2]

        ids_loaded = sem("ids_loaded")
        w0_loaded = sem("w0_loaded")
        w12_loaded = sem("w12_loaded")
        top_loaded = sem("top_loaded")
        w0_folded = sem("w0_folded")
        index_ready = sem("index_ready")
        gathers_begun = sem("gathers_begun")
        rows_gathered = [[sem(f"rows_gathered_{which}_t{t}") for t in range(2)] for which in ("even", "odd")]
        x0_stored = [sem(f"x0_stored_t{t}") for t in range(2)]
        x0_loaded = [sem(f"x0_loaded_t{t}") for t in range(2)]
        h_loaded = [sem(f"h_loaded_t{t}") for t in range(2)]
        mixed_loaded = [sem(f"mixed_loaded_t{t}") for t in range(2)]
        x_stored = [sem(f"x{n + 1}_stored") for n in range(2)]
        x_loaded = [[sem(f"x{n + 1}_loaded_t{t}") for t in range(2)] for n in range(2)]
        x0_copied = sem("x0_copied")
        z_vector_ready = sem("z_vector_ready")
        z_start_ready = sem("z_start_ready")
        z_vector_used = sem("z_vector_used")
        z_pool_ready = sem("z_pool_ready")
        z_pool_used = sem("z_pool_used")
        x_ready = [sem(f"x{n + 1}_ready") for n in range(3)]
        x_summed = [sem(f"x{n + 1}_summed") for n in range(3)]
        early_in_ready = sem("early_in_ready")
        early_summed = sem("early_summed")
        early_ready = sem("early_ready")
        late_in_ready = sem("late_in_ready")
        late1_summed = sem("late1_summed")
        late2_summed = sem("late2_summed")
        late3_summed = sem("late3_summed")
        late1_by_scalar = sem("late1_by_scalar")
        late1_by_vector = sem("late1_by_vector")
        late2_by_scalar = sem("late2_by_scalar")
        late2_by_vector = sem("late2_by_vector")
        y_ready = sem("y_ready")
        y_stored = sem("y_stored")

        block = ctx.enter_context(nc.Block())

        @block.sync
        def _(sp):
            def store_x0(parity, gathered, loaded_before=None, mixed_before=None, tiles=(0, 1)):
                for t in tiles:
                    if loaded_before is not None:
                        sp.wait_ge(x0_loaded[t], loaded_before)
                        sp.wait_ge(h_loaded[t], loaded_before)
                        sp.wait_ge(mixed_loaded[t], mixed_before)
                    sp.wait_ge(rows_gathered[parity][t], gathered)
                    sp.dma_start(x0_dram[parity, t].rearrange("(g m) (b d) -> (m b) g d", m=4, d=D),
                                 gathered_rows[parity][:, t]).then_inc(x0_stored[t], 16)

            def load_h(parity, t):
                sp.dma_start(h_forms[:, t, 0:NH].rearrange("p j c -> p (j c)"),
                             x0_dram[parity, t].rearrange("(h j) c -> h (j c)", j=NH)
                             .unsqueeze(0).broadcast_to([8, 16, NH * C])).then_inc(h_loaded[t], 16)

            def load_mixed(parity, t):
                rows = x0_dram[parity, t].rearrange("(m q) c -> q m c", q=4)
                for s in range(2):
                    half = slice(64 * s, 64 * s + 64)
                    sp.dma_start(x0_mixed[half, t], rows[2 + s].unsqueeze(1).broadcast_to([8, 8, C])
                                 ).then_inc(mixed_loaded[t], 16)
                    sp.dma_start(h_forms[half, t, NH], rows[2 + s].unsqueeze(0).broadcast_to([8, 8, C])
                                 ).then_inc(mixed_loaded[t], 16)

            def load_x0(parity, t, slot):
                sp.dma_start(x0_forms[:, slot, t].rearrange("p i c -> p (i c)"),
                             x0_dram[parity, t].rearrange("(m i) c -> m (i c)", i=NI)
                             .unsqueeze(1).broadcast_to([8, 16, NI * C])).then_inc(x0_loaded[t], 16)

            def store_x(n, pairs):
                sp.wait_ge(x_ready[n], pairs)
                sp.dma_start(x_dram[n], x_sb[n][:]).then_inc(x_stored[n], 16)

            def load_x(n, pairs_16, forms=None):
                forms = x_forms[n] if forms is None else forms
                sp.wait_ge(x_stored[n], pairs_16)
                for t in range(2):
                    sp.dma_start(forms[:, t].rearrange("p j c -> p (j c)"),
                                 x_dram[n][K * t:K * t + K].rearrange("(h j) c -> h (j c)", j=NJ)
                                 .unsqueeze(0).broadcast_to([8, 16, NJ * C])).then_inc(x_loaded[n][t], 16)

            def x_reread(n, pairs_16):
                for t in range(2):
                    sp.wait_ge(x_loaded[n][t], pairs_16)

            sp.dma_start(ids_all[:], ids).then_inc(ids_loaded, 16)
            gathered = 16 * G
            for t in range(2):
                store_x0(0, gathered, tiles=(t,))
                sp.wait_ge(x0_stored[t], 16)
                load_h(0, t)
                load_x0(0, t, 0)
            for t in range(2):
                load_mixed(0, t)

            store_x0(1, gathered, tiles=(0,))
            sp.wait_ge(x0_copied, 1)
            sp.wait_ge(x0_stored[0], 2 * 16)
            load_x0(1, 0, 1)
            sp.wait_ge(z_vector_ready, 3)
            load_mixed(1, 0)
            store_x0(1, gathered, tiles=(1,))
            sp.wait_ge(z_vector_ready, UNITS)
            load_h(1, 0)
            sp.wait_ge(x0_stored[1], 2 * 16)
            load_h(1, 1)
            load_x0(1, 1, 1)
            store_x(0, 1)
            load_mixed(1, 1)
            load_x(0, 16, x_forms[1])
            store_x0(0, 2 * gathered, loaded_before=16, mixed_before=MIXED)
            x_reread(0, 16)
            store_x(0, 2)
            load_x(0, 2 * 16)
            sp.wait_ge(z_vector_ready, 2 * UNITS)
            for t in range(2):
                sp.wait_ge(x0_stored[t], 3 * 16)
                load_h(0, t)
                load_x0(0, t, 2)
            for t in range(2):
                load_mixed(0, t)

            store_x(1, 1)
            sp.wait_ge(z_vector_ready, 3 * UNITS)
            sp.wait_ge(z_pool_ready, UNITS)
            load_x(1, 16)
            store_x0(1, 2 * gathered, loaded_before=2 * 16, mixed_before=2 * MIXED)

            def step(p, parity, load_next=True, store_second_next=True):
                held = (lambda x: x) if isinstance(p, int) else (lambda x: sp.snap(sp.to_reg(x)))
                slot = held((p + 1) % SLOTS)
                next_parity, mixed_there = 1 - parity, held(MIXED * (p + 1))
                this, next_ = held(p), held(p + 1)
                vector_before, pool_before = held(vector_units_before(p)), held(pool_units_before(p))
                vector_layer_2 = held(vector_units_before(p) + 2 * UNITS)
                pool_layer_2 = held(pool_units_before(p) + UNITS)
                p_16, p1_16, p2_16, last_16 = (held(16 * (p + k)) for k in (0, 1, 2, -1))
                rows_there = held(gathered * ((p - parity) // 2 + 2))

                x_reread(0, p_16)
                store_x(0, next_)
                sp.wait_ge(z_vector_ready, vector_before)
                sp.wait_ge(z_pool_ready, pool_before)
                load_x(0, p1_16)
                x_reread(1, last_16)
                store_x(1, this)
                sp.wait_ge(z_vector_ready, vector_layer_2)
                sp.wait_ge(z_pool_ready, pool_layer_2)
                if load_next:
                    for t in range(2):
                        sp.wait_ge(x0_stored[t], p2_16)
                        load_h(next_parity, t)
                        load_x0(next_parity, t, slot)
                    for t in range(2):
                        load_mixed(next_parity, t)
                load_x(1, p_16)
                if store_second_next:
                    store_x0(parity, rows_there, loaded_before=p1_16, mixed_before=mixed_there)

            with sp.Fori(2, NP - 3, 2) as p:
                step(p, 0)
                step(p + 1, 1)
            step(NP - 2, 0, store_second_next=False)
            step(NP - 1, 1, load_next=False, store_second_next=False)

            x_reread(1, 16 * (NP - 1))
            store_x(1, NP)
            sp.wait_ge(z_vector_ready, vector_units_before(NP) + UNITS)
            sp.wait_ge(z_pool_ready, pool_units_before(NP) + UNITS)
            load_x(1, 16 * NP)

            for k, samples in enumerate((slice(0, EARLY * 2 * TB), slice(EARLY * 2 * TB, B))):
                sp.wait_ge(y_ready, k + 1)
                sp.dma_start(out[samples].rearrange("b o -> o b"), y_sb[:, samples]).then_inc(y_stored, 16)
            sp.wait_ge(y_stored, 32)

        @block.gpsimd
        def _(pool):
            def new_index(p, parity):
                if not (isinstance(p, int) and p < 2):
                    for t in range(2):
                        pool.wait_ge(x0_stored[t], 16 * (p - 1))
                nc.gpsimd.tensor_tensor(row_index[parity][:], ids_all[:, p], table_base[:], ALU.add
                                        ).then_inc(index_ready, 1)
                pool.wait_ge(index_ready, p + 1)
                pool.sem_inc(gathers_begun, 1)

            def gather(t, parity):
                for g in range(G):
                    at = t * G + g
                    nc.gpsimd.indirect_dma_start(
                        gathered_rows[parity][:, t, g], None, table,
                        bass.IndirectOffsetOnAxis(ap=row_index[parity][:, at:at + 1], axis=0)
                    ).then_inc(rows_gathered[parity][t], 16)

            def products(n, p, slot, before, first=False, forms=None):
                forms = x_forms[n] if forms is None else forms
                for u in range(UNITS):
                    half, t = divmod(u, 2)
                    if half == 0:
                        pool.wait_ge(x_loaded[n][t], 16 * (p + 1))
                    if not first:
                        pool.wait_ge(z_pool_used, before + u - UNITS + 1)
                    nc.gpsimd.tensor_tensor(
                        z_pool[:, u],
                        x0_forms[:, slot, t, half::2],
                        forms[:, t, NJ - 1].unsqueeze(1).broadcast_to([128, 2, C]),
                        ALU.mult).then_inc(z_pool_ready, 1)

            pool.wait_ge(ids_loaded, 32)
            for p in range(3):
                new_index(p, p % 2)
                gather(0, p % 2)
                gather(1, p % 2)
            new_index(3, 1)
            gather(0, 1)
            products(0, 0, 0, 0, first=True, forms=x_forms[1])
            products(0, 1, 1, UNITS)
            gather(1, 1)

            def step(p, parity, slot, last_slot, gather_second_next=True):
                products(1, p - 2, last_slot, pool_units_before(p))
                if gather_second_next:
                    new_index(p + 2, parity)
                    gather(0, parity)
                products(0, p, slot, pool_units_before(p) + UNITS)
                if gather_second_next:
                    gather(1, parity)

            with pool.Fori(2, NP - 3, 2) as first:
                for parity in range(2):
                    p = first + parity
                    step(p, parity, pool.snap(p % SLOTS), pool.snap((p - 2) % SLOTS))
            for p in (NP - 2, NP - 1):
                step(p, p % 2, p % SLOTS, (p - 2) % SLOTS, gather_second_next=False)
            for n in range(2):
                products(1, NP - 2 + n, (NP - 2 + n) % SLOTS, pool_units_before(NP) + n * UNITS)

        @block.scalar
        def _(act):
            def relu(n, p, consumed):
                act.wait_ge(z_vector_used if n == 0 else z_pool_used, consumed)
                act.wait_ge(x_summed[n], p + COUNT_0[n])
                if n < 2:
                    act.wait_ge(x_stored[n], 16 * p)
                nc.scalar.activation(x_sb[n][:], result[n][:], ACT.Relu).then_inc(x_ready[n], 1)

            def copies(slot, before, layer_0=None, relus=(), first=False, between={}):
                for u in range(UNITS):
                    half, t = divmod(u, 2)
                    if half == 0 and layer_0 is not None:
                        act.wait_ge(x0_loaded[t], 16 * (layer_0 + 1))
                    if not (first and u < 2):
                        act.wait_ge(z_vector_ready, before + u - 1)
                    if half == 1 and layer_0 is not None:
                        nc.scalar.activation(x0_psum[:, t, 0], x0_forms[:, slot, t, 1], ACT.Copy)
                        act.wait_ge(mixed_loaded[t], MIXED * (layer_0 + 1))
                        nc.scalar.activation(x0_psum[:, t, 1], x0_mixed[:, t], ACT.Copy).then_inc(x0_copied, 1)
                    else:
                        nc.scalar.activation(x0_psum[:, t], x0_forms[:, slot, t, half::2],
                                             ACT.Copy).then_inc(x0_copied, 1)
                    if u == 2:
                        for r in relus:
                            relu(*r)
                    if u in between:
                        between[u]()

            act.dma_start(table_base[:], base).then_inc(ids_loaded, 16)
            act.sem_inc(x_ready[2], COUNT_0[2])
            act.dma_start(w0_plain[:], w0).then_inc(w0_loaded, 16)
            act.dma_start(w0_extra[:], w0_mirror).then_inc(w0_loaded, 16)
            act.dma_start(fold_odd[:], odd_h16).then_inc(w0_loaded, 16)
            act.dma_start(w12_sb[:], w12).then_inc(w12_loaded, 16)
            act.dma_start(w_top1_sb[:, 0], w_top1[0:128]).then_inc(top_loaded, 16)
            act.dma_start(w_top1_sb[0:K + D, 1], w_top1[128:128 + K + D]).then_inc(top_loaded, 16)
            act.dma_start(top_in[K:K + D, 1], dense).then_inc(top_loaded, 16)
            act.dma_start(w_top2_sb[:], w_top2).then_inc(top_loaded, 16)
            act.dma_start(w_top3_sb[:], w_top3).then_inc(top_loaded, 16)
            act.dma_start(b_top1_sb[:], b_top1).then_inc(top_loaded, 16)
            act.dma_start(b_top2_sb[:], b_top2).then_inc(top_loaded, 16)

            copies(0, 0, layer_0=0, first=True)
            relu(0, 0, 2)
            copies(1, UNITS, layer_0=1)
            copies(0, 2 * UNITS, relus=[(0, 1, 4)])
            copies(1, 3 * UNITS, relus=[(1, 0, UNITS)])

            with act.Fori(2, NP, SLOTS) as first:
                for k in range(SLOTS):
                    p, slot = first + k, (2 + k) % SLOTS
                    before, pool_before = vector_units_before(p), pool_units_before(p)
                    copies(slot, before, layer_0=p)
                    copies((slot - 2) % SLOTS, before + UNITS,
                           relus=[(0, p, slots_before(p) + 2), (1, p - 1, pool_before)])
                    copies(slot, before + 2 * UNITS, relus=[(2, p - 2, pool_before + UNITS)])

            def top_block(n, t, pairs, ready):
                nc.scalar.activation(top_in[K * (n % 2):K * (n % 2) + K, n // 2, t, TB * pairs[0]:TB * pairs[1]],
                                     d_sums[K * t:K * t + K, n, TB * pairs[0]:TB * pairs[1]],
                                     ACT.Copy).then_inc(ready, 1)

            def y_out(pairs, bank):
                nc.scalar.activation(
                    y_sb.rearrange("o (p t b) -> o t p b", t=2, b=TB)[:, :, pairs[0]:pairs[1]],
                    bank[0:1, 0:(pairs[1] - pairs[0]) * 2 * TB].rearrange("o (t p b) -> o t p b", t=2, b=TB),
                    ACT.Copy).then_inc(y_ready, 1)

            def early_inputs():
                for n in range(3):
                    act.wait_ge(x_summed[n], EARLY + COUNT_0[n])
                    for t in range(2):
                        top_block(n, t, (0, EARLY), early_in_ready)

            def early(k):
                act.wait_ge(early_summed, k + 1)
                bank = early_banks[k % 3]
                if k < N1:
                    nc.scalar.activation(hidden1[:, k, 0:EARLY * 2 * TB], bank[:, 0:EARLY * 2 * TB], ACT.Relu,
                                         bias=b_top1_sb[:, k:k + 1]).then_inc(early_ready, 1)
                elif k < N1 + N2:
                    nc.scalar.activation(hidden2[:, k - N1, 0:EARLY * 2 * TB], bank[:, 0:EARLY * 2 * TB], ACT.Relu,
                                         bias=b_top2_sb[:, k - N1:k - N1 + 1]).then_inc(early_ready, 1)
                else:
                    y_out((0, EARLY), bank)

            act.wait_ge(top_loaded, 16 * 7)
            before, pool_before = vector_units_before(NP), pool_units_before(NP)
            copies((NP - 2) % SLOTS, before, relus=[(1, NP - 1, pool_before)], between={1: early_inputs})
            copies((NP - 1) % SLOTS, before + UNITS, relus=[(2, NP - 2, pool_before + UNITS)],
                   between={0: lambda: early(0), 1: lambda: early(1)})
            for n in range(2):
                act.wait_ge(x_summed[n], NP)
                for t in range(2):
                    top_block(n, t, (EARLY, NP), late_in_ready)
            for k in range(2, N1 + 1):
                early(k)
            relu(2, NP - 1, pool_before + 2 * UNITS)
            act.wait_ge(x_summed[2], NP + COUNT_0[2])
            top_block(2, 0, (EARLY, NP), late_in_ready)
            early(N1 + 1)
            act.wait_ge(late1_summed, 1)
            for k in range(N1 // 2):
                nc.scalar.activation(late1[:, k], late1_psum[0][:, k], ACT.Relu,
                                     bias=b_top1_sb[:, k:k + 1]).then_inc(late1_by_scalar, 1)
            early(N1 + N2)
            act.wait_ge(late2_summed, 1)
            nc.scalar.activation(late2[:, 0], late2_psum[0][:, 0:LATE], ACT.Relu,
                                 bias=b_top2_sb[:, 0:1]).then_inc(late2_by_scalar, 1)
            act.wait_ge(late3_summed, 1)
            y_out((EARLY, NP), late3_psum)

        @block.vector
        def _(dve):
            def sum_d(n, p):
                dve.wait_ge(x_ready[n], p + 1 + COUNT_0[n])
                nc.vector.tensor_reduce(d_sums[:, n, bass.ds(p * TB, TB)],
                                        x_sb[n][:].rearrange("p (b d) -> p b d", d=D),
                                        AXIS.X, ALU.add).then_inc(x_summed[n], 1)

            def may_multiply(copied, used):
                dve.wait_ge(x0_copied, copied)
                if used is not None:
                    dve.wait_ge(z_vector_used, used)

            def unit(z, left, right, copied, used):
                may_multiply(copied, used)
                nc.vector.tensor_tensor(z, left, right, ALU.mult).then_inc(z_vector_ready, 1)

            def layer_0(p, before, filled, start=0):
                for u in range(UNITS):
                    half, t = divmod(u, 2)
                    z = z_vector[:, ring_slot(start + t)]
                    if half == 0:
                        dve.wait_ge(h_loaded[t], 16 * (p + 1))
                        may_multiply(before + u + 1, must_be_used(filled, t))
                        nc.vector.tensor_tensor(z[:, 2], x0_psum[:, t, 1], h_forms[:, t, 1], ALU.mult)
                        nc.vector.tensor_tensor(z[:, 0:2], x0_psum[:, t, 0].unsqueeze(1).broadcast_to([128, 2, C]),
                                                h_forms[:, t, 0:2], ALU.mult).then_inc(z_vector_ready, 1)
                    else:
                        dve.wait_ge(mixed_loaded[t], MIXED * (p + 1))
                        unit(z[:, 3:5], x0_psum[:, t], h_forms[:, t, 1:3], before + u + 1, None)

            def layer(n, p, before, filled, start, forms=None):
                forms = x_forms[n] if forms is None else forms
                for u in range(UNITS):
                    t = u % 2
                    if u < 2:
                        dve.wait_ge(x_loaded[n][t], 16 * (p + 1))
                    z = z_vector[:, ring_slot(start + u)].rearrange("p (j i) c -> p j i c", i=2)
                    may_multiply(before + u + 1, must_be_used(filled, u))
                    for j, j_end in ((0, 1), (1, JV)) if u == 1 else ((0, JV),):
                        done = nc.vector.tensor_tensor(
                            z[:, j:j_end],
                            x0_psum[:, t].unsqueeze(1).broadcast_to([128, j_end - j, 2, C]),
                            forms[:, t, j:j_end].unsqueeze(2).broadcast_to([128, j_end - j, 2, C]), ALU.mult)
                        done.then_inc(z_vector_ready if j_end == JV else z_start_ready, 1)

            def must_be_used(filled, k):
                if isinstance(filled, int) and filled + k < RING:
                    return None
                return filled + k - RING + 1

            dve.sem_inc(x_summed[2], COUNT_0[2])
            dve.wait_ge(w0_loaded, 48)
            nc.vector.tensor_tensor(w0_plain[:, 1:3], w0_plain[:, 1:3], w0_extra[:, 1:3], ALU.add
                                    ).then_inc(w0_folded, 1)
            for c in (0, 3):
                nc.vector.scalar_tensor_tensor(w0_plain[:, c], w0_extra[:, c], fold_odd[:, 0:1], w0_plain[:, c],
                                               ALU.mult, ALU.add).then_inc(w0_folded, 1)
            layer_0(0, 0, 0, -12)
            layer_0(1, UNITS, 2, -10)
            sum_d(0, 0)
            layer(0, 0, 2 * UNITS, 4, -8, forms=x_forms[1])
            sum_d(0, 1)
            layer(0, 1, 3 * UNITS, 8, -4)
            sum_d(1, 0)
            with dve.Fori(2, NP) as p:
                before, filled = vector_units_before(p), slots_before(p)
                layer_0(p, before, filled)
                layer(1, p - 2, before + UNITS, filled + 2, 2)
                sum_d(0, p)
                sum_d(1, p - 1)
                layer(0, p, before + 2 * UNITS, filled + 2 + UNITS, 2 + UNITS)
                sum_d(2, p - 2)
            layer(1, NP - 2, vector_units_before(NP), slots_before(NP), 0)
            sum_d(1, NP - 1)
            layer(1, NP - 1, vector_units_before(NP) + UNITS, slots_before(NP) + UNITS, UNITS)
            sum_d(2, NP - 2)
            sum_d(2, NP - 1)

            dve.wait_ge(x_summed[2], NP + COUNT_0[2])
            nc.vector.tensor_copy(top_in[0:K, 1, 1, TB * EARLY:TB * NP],
                                  d_sums[K:2 * K, 2, TB * EARLY:TB * NP]).then_inc(late_in_ready, 1)
            dve.wait_ge(late1_summed, 2)
            for k in range(N1 // 2, N1):
                nc.vector.tensor_scalar(late1[:, k], late1_psum[1][:, k - N1 // 2], b_top1_sb[:, k:k + 1], 0.0,
                                        ALU.add, ALU.max).then_inc(late1_by_vector, 1)
            dve.wait_ge(late2_summed, 2)
            nc.vector.tensor_scalar(late2[:, 1], late2_psum[1][:, 0:LATE], b_top2_sb[:, 1:2], 0.0,
                                    ALU.add, ALU.max).then_inc(late2_by_vector, 1)

        @block.tensor
        def _(pe):
            def side_by_side(n, weights, z, slots, first, last):
                for t in range(2):
                    done = nc.tensor.matmul(result[n][K * t:K * t + K], weights, z[:, slots[t]],
                                            start=first, stop=last)
                return done

            def layer_0(p, before, start=0):
                slots = ring_slot(start), ring_slot(start + 1)
                if not (isinstance(p, int) and p == 0):
                    pe.wait_ge(x_ready[0], p)
                for half in range(2):
                    pe.wait_ge(z_vector_ready, before + 2 * half + 2)
                    for c in range(CH0[half]):
                        done = side_by_side(0, w0_plain[:, CH0[0] * half + c], z_vector[:, :, CH0[0] * half + c],
                                            slots, half == 0 and c == 0, half == 1 and c == CH0[1] - 1)
                done.then_inc(z_vector_used, 2)

            def layer(n, p, before, starts, pool_before, start, between={}):
                if not (isinstance(p, int) and p == 0):
                    pe.wait_ge(x_ready[n + 1], p + COUNT_0[n + 1])
                for half in range(2):
                    slots = ring_slot(start + 2 * half), ring_slot(start + 2 * half + 1)
                    if half == 0:
                        pe.wait_ge(z_vector_ready, before + 1)
                        pe.wait_ge(z_start_ready, starts + 1)
                    for c in range(JV * 2):
                        if (half, c) in ((0, 2), (1, 0)):
                            pe.wait_ge(z_vector_ready, before + 2 * half + 2)
                        done = side_by_side(n + 1, w12_sb[:, n, c // 2, half + 2 * (c % 2)],
                                            z_vector[:, :, c], slots, half == 0 and c == 0, False)
                    done.then_inc(z_vector_used, 2)
                    for k in between.get((half, "vector"), ()):
                        early(k)
                    pe.wait_ge(z_pool_ready, pool_before + 2 * half + 2)
                    for c in range(2):
                        done = side_by_side(n + 1, w12_sb[:, n, NJ - 1, half + 2 * c],
                                            z_pool[:, :, c], (2 * half, 2 * half + 1), False, half == 1 and c == 1)
                    done.then_inc(z_pool_used, 2)
                    for k in between.get((half, "pool"), ()):
                        early(k)

            def early(k):
                if k == 0:
                    pe.wait_ge(top_loaded, 16 * 7)
                    pe.wait_ge(early_in_ready, 6)
                if k == 2:
                    pe.wait_ge(x_ready[1], NP)
                if k >= 3:
                    pe.wait_ge(early_ready, k - 2)
                bank = early_banks[k % 3]
                if k < N1:
                    for half, rows in enumerate((128, K + D)):
                        done = nc.tensor.matmul(
                            bank[:, 0:EARLY * 2 * TB], w_top1_sb[0:rows, half, 128 * k:128 * k + 128],
                            top_in[0:rows, half, :, 0:EARLY * TB], start=half == 0, stop=half == 1)
                elif k < N1 + N2:
                    pe.wait_ge(early_ready, N1)
                    for n in range(N1):
                        done = nc.tensor.matmul(
                            bank[:, 0:EARLY * 2 * TB], w_top2_sb[:, n, 128 * (k - N1):128 * (k - N1) + 128],
                            hidden1[:, n], start=n == 0, stop=n == N1 - 1)
                else:
                    pe.wait_ge(early_ready, N1 + N2)
                    for n in range(N2):
                        done = nc.tensor.matmul(bank[0:1, 0:EARLY * 2 * TB], w_top3_sb[:, n:n + 1],
                                                hidden2[:, n], start=n == 0, stop=n == N2 - 1)
                done.then_inc(early_summed, 1)

            pe.wait_ge(w0_loaded, 48)
            pe.wait_ge(w0_folded, 3)
            layer_0(0, 0, -12)
            layer_0(1, UNITS, -10)
            pe.wait_ge(w12_loaded, 16)
            layer(0, 0, 2 * UNITS, 0, 0, -8)
            layer(0, 1, 3 * UNITS, 1, UNITS, -4)
            with pe.Fori(2, NP) as p:
                before, pool_before = vector_units_before(p), pool_units_before(p)
                layer_0(p, before)
                layer(1, p - 2, before + UNITS, starts_before(p), pool_before, 2)
                layer(0, p, before + 2 * UNITS, starts_before(p) + 1, pool_before + UNITS, 2 + UNITS)
            before, pool_before = vector_units_before(NP), pool_units_before(NP)
            layer(1, NP - 2, before, starts_before(NP), pool_before, 0, {(0, "vector"): [0], (0, "pool"): [1]})
            layer(1, NP - 1, before + UNITS, starts_before(NP) + 1, pool_before + UNITS, UNITS,
                  {(0, "vector"): [2], (0, "pool"): [3], (1, "vector"): [N1]})
            early(N1 + 1)

            pe.wait_ge(late_in_ready, 6)
            pe.wait_ge(z_vector_ready, before + 2 * UNITS)
            for k in range(N1):
                for half, rows in enumerate((128, K + D)):
                    done = nc.tensor.matmul(
                        late1_psum[k // 2][:, k % 2], w_top1_sb[0:rows, half, 128 * k:128 * k + 128],
                        top_in[0:rows, half, :, EARLY * TB:NP * TB], start=half == 0, stop=half == 1)
                if k % 2:
                    done.then_inc(late1_summed, 1)
            early(N1 + N2)
            for m in range(N2):
                for k in range(N1):
                    if k < N1 // 2:
                        pe.wait_ge(late1_by_scalar, k + 1)
                    else:
                        pe.wait_ge(late1_by_vector, k - N1 // 2 + 1)
                    done = nc.tensor.matmul(late2_psum[m][:, 0:LATE], w_top2_sb[:, k, 128 * m:128 * m + 128],
                                            late1[:, k], start=k == 0, stop=k == N1 - 1)
                done.then_inc(late2_summed, 1)
            pe.wait_ge(late2_by_scalar, 1)
            nc.tensor.matmul(late3_psum[0:1, 0:LATE], w_top3_sb[:, 0:1], late2[:, 0], start=True, stop=False)
            pe.wait_ge(late2_by_vector, 1)
            nc.tensor.matmul(late3_psum[0:1, 0:LATE], w_top3_sb[:, 1:2], late2[:, 1],
                             start=False, stop=True).then_inc(late3_summed, 1)


def kernel(**inputs):
    import concourse.bacc as bacc
    from concourse.bass_utils import run_bass_kernel_spmd

    a = {name: np.asarray(x) for name, x in inputs.items()}
    tables = [a[f"tbl_{m}"] for m in range(M)]
    starts = np.cumsum([0] + [t.shape[0] for t in tables[:-1]]).astype(np.int32)
    base = np.tile(np.repeat(starts.reshape(G, 4).T, TB, axis=0), (1, 2))
    ids = a["ids"].reshape(NP, 2, TB, G, 4).transpose(4, 2, 0, 1, 3).reshape(128, NP, 2 * G)

    def chunks(w, nj):
        return w.reshape(8, NI, 16, nj, K).transpose(0, 2, 3, 1, 4).reshape(128, nj, NI, K)

    w0 = a["L0_rec_W0"]
    plain, mirror = chunks(w0, NH), chunks(w0.transpose(1, 0, 2), NH)
    mixed = [w0[2 + s::4, 2 + s::4].reshape(64, K) for s in range(2)]
    w0_used = np.stack([plain[:, 0, 0], plain[:, 1, 0], plain[:, 1, 2], plain[:, 1, 1], np.concatenate(mixed)],
                       axis=1)
    w0_mirror = np.stack([mirror[:, 0, 0], mirror[:, 1, 0], mirror[:, 1, 2], mirror[:, 1, 1]], axis=1)
    odd_h16 = (np.arange(128) % 2).astype(np.float32).reshape(128, 1)
    w12 = np.stack([chunks(a["L0_rec_W1"], NJ), chunks(a["L0_rec_W2"], NJ)], axis=1)
    dense = a["dense_ctx"].reshape(NP, 2, TB, D).transpose(3, 1, 0, 2).reshape(D, 2, NP * TB)
    arrays = {
        "table": np.concatenate(tables, axis=0), "ids": ids, "base": base, "odd_h16": odd_h16,
        "w0": w0_used, "w0_mirror": w0_mirror, "w12": w12, "dense": dense,
        "w_top1": a["W_top1"], "b_top1": a["b_top1"].reshape(N1, 128).T,
        "w_top2": a["W_top2"].reshape(N1, 128, H2).transpose(1, 0, 2),
        "b_top2": a["b_top2"].reshape(N2, 128).T,
        "w_top3": a["W_top3"].reshape(N2, 128).T,
    }
    arrays = {name: np.ascontiguousarray(x) for name, x in arrays.items()}

    nc = bacc.Bacc("TRN2", target_bir_lowering=False, num_devices=1)
    ins = [nc.dram_tensor(name, x.shape, mybir.dt.from_np(x.dtype), kind="ExternalInput").ap()
           for name, x in arrays.items()]
    out = nc.dram_tensor("y", (B, 1), F32, kind="ExternalOutput").ap()
    build(nc, *ins, out)
    return run_bass_kernel_spmd(nc, [arrays], core_ids=[0]).results[0]["y"]
```
